# Optimizing a Trainium2 kernel written in Bass

```python
import numpy as np
import jax
import jax.numpy as jnp

def _softmax(x, axis=-1):
    return jax.nn.softmax(x, axis=axis)

def _gelu(x):
    return jax.nn.gelu(x, approximate=True)

def _silu(x):
    return jax.nn.silu(x)

def _sigmoid(x):
    return jax.nn.sigmoid(x)

def _layernorm(x, axis=-1, eps=1e-05):
    m = jnp.mean(x, axis=axis, keepdims=True)
    v = jnp.var(x, axis=axis, keepdims=True)
    return (x - m) / jnp.sqrt(v + eps)

def _scatter_add(tgt, idx, src, axis=0):
    return tgt.at[idx].add(src)

def _segment_sum(src, seg, n):
    return jax.ops.segment_sum(src, seg, n)
kernel_name = 'mk_conv_preact_d4_conv_nhwc128_r2_472845'

def setup_inputs(seed: int=0):
    np.random.seed(seed)
    _w = jnp.asarray

    def _rec_inputs():
        import jax
        import jax.numpy as jnp
        _gk = jax.random.key(seed)
        x = -0.0003482 + 1 * jax.random.normal(jax.random.fold_in(_gk, 1), (1, 192, 192, 64), jnp.float32)
        return x
    x = _rec_inputs()

    def _L0_conv_setup():
        import jax, jax.numpy as jnp
        import numpy as np
        DIM = 64
        HID = 64
        EPS = 1e-05

        def _layernorm(x, w, b):
            mu = jnp.mean(x, axis=-1, keepdims=True)
            var = jnp.var(x, axis=-1, keepdims=True)
            return (x - mu) * jax.lax.rsqrt(var + EPS) * w + b
        key = jax.random.key(seed)
        ks = jax.random.split(key, 8)
        B, N = (1, 192)
        s_in = 1.0 / np.sqrt(DIM)
        s_hid = 1.0 / np.sqrt(HID)
        return {'x': jax.random.normal(ks[0], (B, N, N, DIM), dtype=jnp.float32), 'mask': jnp.ones((B, N, N), dtype=jnp.float32), 'ln1_w': jnp.ones((DIM,), jnp.float32), 'ln1_b': jnp.zeros((DIM,), jnp.float32), 'Wl': jax.random.uniform(ks[1], (HID, DIM), jnp.float32, -s_in, s_in), 'Wr': jax.random.uniform(ks[2], (HID, DIM), jnp.float32, -s_in, s_in), 'Wlg': jax.random.uniform(ks[3], (HID, DIM), jnp.float32, -s_in, s_in), 'Wrg': jax.random.uniform(ks[4], (HID, DIM), jnp.float32, -s_in, s_in), 'Wog': jax.random.uniform(ks[5], (HID, DIM), jnp.float32, -s_in, s_in), 'ln2_w': jnp.ones((HID,), jnp.float32), 'ln2_b': jnp.zeros((HID,), jnp.float32), 'Wout': jax.random.uniform(ks[6], (DIM, HID), jnp.float32, -s_hid, s_hid)}
    _L0_conv_all = _L0_conv_setup()
    _L0_conv_in = {k: v for k, v in _L0_conv_all.items() if k in ('mask', 'ln1_w', 'ln1_b', 'Wl', 'Wr', 'Wlg', 'Wrg', 'Wog', 'ln2_w', 'ln2_b', 'Wout')}
    del _L0_conv_all

    def _L1_conv_setup():
        import jax, jax.numpy as jnp
        import numpy as np
        EPS = 1e-05

        def _layernorm(x, w, b):
            mu = jnp.mean(x, axis=-1, keepdims=True)
            var = jnp.mean(jnp.square(x - mu), axis=-1, keepdims=True)
            return (x - mu) * jax.lax.rsqrt(var + EPS) * w + b
        key = jax.random.key(seed)
        ks = jax.random.split(key, 16)
        B, N, C_Z, C_H = (1, 192, 64, 64)
        s_z = 1.0 / np.sqrt(C_Z)
        s_h = 1.0 / np.sqrt(C_H)
        return {'z': jax.random.normal(ks[0], (B, N, N, C_Z), jnp.float32), 'mask': jnp.ones((B, N, N), jnp.float32), 'ln_in_w': jnp.ones((C_Z,), jnp.float32), 'ln_in_b': jnp.zeros((C_Z,), jnp.float32), 'w_a_p': jax.random.normal(ks[1], (C_Z, C_H), jnp.float32) * s_z, 'b_a_p': jnp.zeros((C_H,), jnp.float32), 'w_a_g': jax.random.normal(ks[2], (C_Z, C_H), jnp.float32) * s_z, 'b_a_g': jnp.zeros((C_H,), jnp.float32), 'w_b_p': jax.random.normal(ks[3], (C_Z, C_H), jnp.float32) * s_z, 'b_b_p': jnp.zeros((C_H,), jnp.float32), 'w_b_g': jax.random.normal(ks[4], (C_Z, C_H), jnp.float32) * s_z, 'b_b_g': jnp.zeros((C_H,), jnp.float32), 'w_g': jax.random.normal(ks[5], (C_Z, C_Z), jnp.float32) * s_z, 'b_g': jnp.zeros((C_Z,), jnp.float32), 'ln_out_w': jnp.ones((C_H,), jnp.float32), 'ln_out_b': jnp.zeros((C_H,), jnp.float32), 'w_o': jax.random.normal(ks[6], (C_H, C_Z), jnp.float32) * s_h, 'b_o': jnp.zeros((C_Z,), jnp.float32)}
    _L1_conv_all = _L1_conv_setup()
    _L1_conv_in = {k: v for k, v in _L1_conv_all.items() if k in ('mask', 'ln_in_w', 'ln_in_b', 'w_a_p', 'b_a_p', 'w_a_g', 'b_a_g', 'w_b_p', 'b_b_p', 'w_b_g', 'b_b_g', 'w_g', 'b_g', 'ln_out_w', 'ln_out_b', 'w_o', 'b_o')}
    del _L1_conv_all

    def _L2_conv_setup():
        import jax, jax.numpy as jnp
        import numpy as np
        EPS = 1e-05

        def layer_norm(x, a, b):
            m = jnp.mean(x, axis=-1, keepdims=True)
            v = jnp.var(x, axis=-1, keepdims=True)
            return a * (x - m) / jnp.sqrt(v + EPS) + b
        key = jax.random.key(seed)
        ks = jax.random.split(key, 16)
        b, n, d, h = (1, 192, 64, 64)
        s = 1.0 / np.sqrt(d)
        inp = {'x': jax.random.normal(ks[0], (b, n, n, d), dtype=jnp.float32), 'norm_a': jnp.ones((d,), jnp.float32), 'norm_b': jnp.zeros((d,), jnp.float32), 'Wl': jax.random.normal(ks[1], (d, h), jnp.float32) * s, 'bl': jnp.zeros((h,), jnp.float32), 'Wr': jax.random.normal(ks[2], (d, h), jnp.float32) * s, 'br': jnp.zeros((h,), jnp.float32), 'Wlg': jax.random.normal(ks[3], (d, h), jnp.float32) * s, 'blg': jnp.ones((h,), jnp.float32), 'Wrg': jax.random.normal(ks[4], (d, h), jnp.float32) * s, 'brg': jnp.ones((h,), jnp.float32), 'Wog': jax.random.normal(ks[5], (d, h), jnp.float32) * s, 'bog': jnp.ones((h,), jnp.float32), 'on_a': jnp.ones((h,), jnp.float32), 'on_b': jnp.zeros((h,), jnp.float32), 'Wo': jax.random.normal(ks[6], (h, d), jnp.float32) * s, 'bo': jnp.zeros((d,), jnp.float32)}
        return inp
    _L2_conv_all = _L2_conv_setup()
    _L2_conv_in = {k: v for k, v in _L2_conv_all.items() if k in ('norm_a', 'norm_b', 'Wl', 'bl', 'Wr', 'br', 'Wlg', 'blg', 'Wrg', 'brg', 'Wog', 'bog', 'on_a', 'on_b', 'Wo', 'bo')}
    del _L2_conv_all

    def _L3_conv_setup():
        import jax, jax.numpy as jnp
        import numpy as np
        LN_EPS = 1e-05

        def _layernorm(x, w, b):
            mu = jnp.mean(x, axis=-1, keepdims=True)
            var = jnp.mean(jnp.square(x - mu), axis=-1, keepdims=True)
            return (x - mu) * jax.lax.rsqrt(var + LN_EPS) * w + b
        key = jax.random.key(seed)
        ks = jax.random.split(key, 4)
        b, n, d, h = (1, 192, 64, 64)
        x = jax.random.normal(ks[0], (b, n, n, d), dtype=jnp.float32)
        mask = jnp.ones((b, n), dtype=bool)
        W_lr = jax.random.normal(ks[1], (d, 4 * h), dtype=jnp.float32) * (1.0 / np.sqrt(d))
        W_gate = jax.random.normal(ks[2], (d, h), dtype=jnp.float32) * (1.0 / np.sqrt(d))
        ln_w = jnp.ones((h,), dtype=jnp.float32)
        ln_b = jnp.zeros((h,), dtype=jnp.float32)
        W_out = jax.random.normal(ks[3], (h, d), dtype=jnp.float32) * (1.0 / np.sqrt(h))
        return {'x': x, 'mask': mask, 'W_lr': W_lr, 'W_gate': W_gate, 'ln_w': ln_w, 'ln_b': ln_b, 'W_out': W_out}
    _L3_conv_all = _L3_conv_setup()
    _L3_conv_in = {k: v for k, v in _L3_conv_all.items() if k in ('mask', 'W_lr', 'W_gate', 'ln_w', 'ln_b', 'W_out')}
    del _L3_conv_all
    return {'x': x, 'L0_conv_mask': _L0_conv_in['mask'], 'L0_conv_ln1_w': _L0_conv_in['ln1_w'], 'L0_conv_ln1_b': _L0_conv_in['ln1_b'], 'L0_conv_Wl': _L0_conv_in['Wl'], 'L0_conv_Wr': _L0_conv_in['Wr'], 'L0_conv_Wlg': _L0_conv_in['Wlg'], 'L0_conv_Wrg': _L0_conv_in['Wrg'], 'L0_conv_Wog': _L0_conv_in['Wog'], 'L0_conv_ln2_w': _L0_conv_in['ln2_w'], 'L0_conv_ln2_b': _L0_conv_in['ln2_b'], 'L0_conv_Wout': _L0_conv_in['Wout'], 'L1_conv_mask': _L1_conv_in['mask'], 'L1_conv_ln_in_w': _L1_conv_in['ln_in_w'], 'L1_conv_ln_in_b': _L1_conv_in['ln_in_b'], 'L1_conv_w_a_p': _L1_conv_in['w_a_p'], 'L1_conv_b_a_p': _L1_conv_in['b_a_p'], 'L1_conv_w_a_g': _L1_conv_in['w_a_g'], 'L1_conv_b_a_g': _L1_conv_in['b_a_g'], 'L1_conv_w_b_p': _L1_conv_in['w_b_p'], 'L1_conv_b_b_p': _L1_conv_in['b_b_p'], 'L1_conv_w_b_g': _L1_conv_in['w_b_g'], 'L1_conv_b_b_g': _L1_conv_in['b_b_g'], 'L1_conv_w_g': _L1_conv_in['w_g'], 'L1_conv_b_g': _L1_conv_in['b_g'], 'L1_conv_ln_out_w': _L1_conv_in['ln_out_w'], 'L1_conv_ln_out_b': _L1_conv_in['ln_out_b'], 'L1_conv_w_o': _L1_conv_in['w_o'], 'L1_conv_b_o': _L1_conv_in['b_o'], 'L2_conv_norm_a': _L2_conv_in['norm_a'], 'L2_conv_norm_b': _L2_conv_in['norm_b'], 'L2_conv_Wl': _L2_conv_in['Wl'], 'L2_conv_bl': _L2_conv_in['bl'], 'L2_conv_Wr': _L2_conv_in['Wr'], 'L2_conv_br': _L2_conv_in['br'], 'L2_conv_Wlg': _L2_conv_in['Wlg'], 'L2_conv_blg': _L2_conv_in['blg'], 'L2_conv_Wrg': _L2_conv_in['Wrg'], 'L2_conv_brg': _L2_conv_in['brg'], 'L2_conv_Wog': _L2_conv_in['Wog'], 'L2_conv_bog': _L2_conv_in['bog'], 'L2_conv_on_a': _L2_conv_in['on_a'], 'L2_conv_on_b': _L2_conv_in['on_b'], 'L2_conv_Wo': _L2_conv_in['Wo'], 'L2_conv_bo': _L2_conv_in['bo'], 'L3_conv_mask': _L3_conv_in['mask'], 'L3_conv_W_lr': _L3_conv_in['W_lr'], 'L3_conv_W_gate': _L3_conv_in['W_gate'], 'L3_conv_ln_w': _L3_conv_in['ln_w'], 'L3_conv_ln_b': _L3_conv_in['ln_b'], 'L3_conv_W_out': _L3_conv_in['W_out']}

def reference(x, L0_conv_mask, L0_conv_ln1_w, L0_conv_ln1_b, L0_conv_Wl, L0_conv_Wr, L0_conv_Wlg, L0_conv_Wrg, L0_conv_Wog, L0_conv_ln2_w, L0_conv_ln2_b, L0_conv_Wout, L1_conv_mask, L1_conv_ln_in_w, L1_conv_ln_in_b, L1_conv_w_a_p, L1_conv_b_a_p, L1_conv_w_a_g, L1_conv_b_a_g, L1_conv_w_b_p, L1_conv_b_b_p, L1_conv_w_b_g, L1_conv_b_b_g, L1_conv_w_g, L1_conv_b_g, L1_conv_ln_out_w, L1_conv_ln_out_b, L1_conv_w_o, L1_conv_b_o, L2_conv_norm_a, L2_conv_norm_b, L2_conv_Wl, L2_conv_bl, L2_conv_Wr, L2_conv_br, L2_conv_Wlg, L2_conv_blg, L2_conv_Wrg, L2_conv_brg, L2_conv_Wog, L2_conv_bog, L2_conv_on_a, L2_conv_on_b, L2_conv_Wo, L2_conv_bo, L3_conv_mask, L3_conv_W_lr, L3_conv_W_gate, L3_conv_ln_w, L3_conv_ln_b, L3_conv_W_out):
    import jax
    import jax.numpy as jnp

    def _L0_conv_ref(x, mask, ln1_w, ln1_b, Wl, Wr, Wlg, Wrg, Wog, ln2_w, ln2_b, Wout):
        import jax, jax.numpy as jnp
        import numpy as np
        DIM = 64
        HID = 64
        EPS = 1e-05

        def _layernorm(x, w, b):
            mu = jnp.mean(x, axis=-1, keepdims=True)
            var = jnp.var(x, axis=-1, keepdims=True)
            return (x - mu) * jax.lax.rsqrt(var + EPS) * w + b
        xn = _layernorm(x, ln1_w, ln1_b)
        m = mask[..., None]
        left = xn @ Wl.T * m * jax.nn.sigmoid(xn @ Wlg.T)
        right = xn @ Wr.T * m * jax.nn.sigmoid(xn @ Wrg.T)
        out_gate = jax.nn.sigmoid(xn @ Wog.T)
        out = jnp.einsum('bikd,bjkd->bijd', left.astype(jnp.bfloat16), right.astype(jnp.bfloat16)).astype(jnp.float32)
        out = _layernorm(out, ln2_w, ln2_b) * out_gate
        return out @ Wout.T

    def _L1_conv_ref(z, mask, ln_in_w, ln_in_b, w_a_p, b_a_p, w_a_g, b_a_g, w_b_p, b_b_p, w_b_g, b_b_g, w_g, b_g, ln_out_w, ln_out_b, w_o, b_o):
        import jax, jax.numpy as jnp
        import numpy as np
        EPS = 1e-05

        def _layernorm(x, w, b):
            mu = jnp.mean(x, axis=-1, keepdims=True)
            var = jnp.mean(jnp.square(x - mu), axis=-1, keepdims=True)
            return (x - mu) * jax.lax.rsqrt(var + EPS) * w + b
        m = mask[..., None]
        x = _layernorm(z, ln_in_w, ln_in_b)
        a = m * jax.nn.sigmoid(x @ w_a_g + b_a_g) * (x @ w_a_p + b_a_p)
        b = m * jax.nn.sigmoid(x @ w_b_g + b_b_g) * (x @ w_b_p + b_b_p)
        t = jnp.einsum('bikc,bjkc->bijc', a, b)
        t = _layernorm(t, ln_out_w, ln_out_b) @ w_o + b_o
        g = jax.nn.sigmoid(x @ w_g + b_g)
        return g * t

    def _L2_conv_ref(x, norm_a, norm_b, Wl, bl, Wr, br, Wlg, blg, Wrg, brg, Wog, bog, on_a, on_b, Wo, bo):
        import jax, jax.numpy as jnp
        import numpy as np
        EPS = 1e-05

        def layer_norm(x, a, b):
            m = jnp.mean(x, axis=-1, keepdims=True)
            v = jnp.var(x, axis=-1, keepdims=True)
            return a * (x - m) / jnp.sqrt(v + EPS) + b
        n = x.shape[1]
        xn = layer_norm(x, norm_a, norm_b)
        left = (xn @ Wl + bl) * jax.nn.sigmoid(xn @ Wlg + blg)
        right = (xn @ Wr + br) * jax.nn.sigmoid(xn @ Wrg + brg)
        out_gate = jax.nn.sigmoid(xn @ Wog + bog)
        out = jnp.einsum('bkjd,bkid->bijd', left.astype(jnp.float32), right.astype(jnp.float32)) / n
        out = out.astype(x.dtype)
        out = layer_norm(out, on_a, on_b) * out_gate
        return out @ Wo + bo

    def _L3_conv_ref(x, mask, W_lr, W_gate, ln_w, ln_b, W_out):
        import jax, jax.numpy as jnp
        import numpy as np
        LN_EPS = 1e-05

        def _layernorm(x, w, b):
            mu = jnp.mean(x, axis=-1, keepdims=True)
            var = jnp.mean(jnp.square(x - mu), axis=-1, keepdims=True)
            return (x - mu) * jax.lax.rsqrt(var + LN_EPS) * w + b
        pm = (mask[:, :, None] & mask[:, None, :])[..., None].astype(x.dtype)
        proj = jnp.einsum('bijd,dh->bijh', x, W_lr)
        val, gate = jnp.split(proj, 2, axis=-1)
        glu = val * jax.nn.sigmoid(gate)
        left, right = jnp.split(glu, 2, axis=-1)
        left = left * pm
        right = right * pm
        out = jnp.einsum('bkjd,bkid->bijd', left, right)
        out = _layernorm(out, ln_w, ln_b)
        out_gate = jax.nn.sigmoid(jnp.einsum('bijd,dh->bijh', x, W_gate))
        return jnp.einsum('bijh,hd->bijd', out, W_out) * out_gate

    def _gn(v, G=32, eps=1e-05):
        B_, H_, W_, C_ = v.shape
        g = v.reshape(B_, H_, W_, G, C_ // G)
        m = jnp.mean(g, axis=(1, 2, 4), keepdims=True)
        s = jnp.var(g, axis=(1, 2, 4), keepdims=True)
        return ((g - m) / jnp.sqrt(s + eps)).reshape(v.shape)

    def _ln_c(v, eps=1e-06):
        m = jnp.mean(v, axis=-1, keepdims=True)
        s = jnp.var(v, axis=-1, keepdims=True)
        return (v - m) / jnp.sqrt(s + eps)

    def _ln_t(v, eps=1e-05):
        m = jnp.mean(v, axis=-1, keepdims=True)
        s = jnp.var(v, axis=-1, keepdims=True)
        return (v - m) / jnp.sqrt(s + eps)

    def _to_tokens(v):
        B_, H_, W_, C_ = v.shape
        return v.reshape(B_, H_ * W_, C_)

    def _from_tokens(t, like):
        return t.reshape(like.shape)
    x = x + _L0_conv_ref(_gn(x), L0_conv_mask, L0_conv_ln1_w, L0_conv_ln1_b, L0_conv_Wl, L0_conv_Wr, L0_conv_Wlg, L0_conv_Wrg, L0_conv_Wog, L0_conv_ln2_w, L0_conv_ln2_b, L0_conv_Wout)
    x = x + _L1_conv_ref(_gn(x), L1_conv_mask, L1_conv_ln_in_w, L1_conv_ln_in_b, L1_conv_w_a_p, L1_conv_b_a_p, L1_conv_w_a_g, L1_conv_b_a_g, L1_conv_w_b_p, L1_conv_b_b_p, L1_conv_w_b_g, L1_conv_b_b_g, L1_conv_w_g, L1_conv_b_g, L1_conv_ln_out_w, L1_conv_ln_out_b, L1_conv_w_o, L1_conv_b_o)
    x = x + _L2_conv_ref(_gn(x), L2_conv_norm_a, L2_conv_norm_b, L2_conv_Wl, L2_conv_bl, L2_conv_Wr, L2_conv_br, L2_conv_Wlg, L2_conv_blg, L2_conv_Wrg, L2_conv_brg, L2_conv_Wog, L2_conv_bog, L2_conv_on_a, L2_conv_on_b, L2_conv_Wo, L2_conv_bo)
    x = x + _L3_conv_ref(_gn(x), L3_conv_mask, L3_conv_W_lr, L3_conv_W_gate, L3_conv_ln_w, L3_conv_ln_b, L3_conv_W_out)
    return x

_drawn_inputs = setup_inputs


def setup_inputs(seed=0):
    import zlib

    import numpy as np

    out = dict(_drawn_inputs(seed))
    spreads = {'L0_conv_ln1_w': (1.0, 0.2),
     'L0_conv_ln1_b': (0.0, 0.1),
     'L0_conv_ln2_w': (1.0, 0.2),
     'L0_conv_ln2_b': (0.0, 0.1),
     'L1_conv_ln_in_w': (1.0, 0.2),
     'L1_conv_ln_in_b': (0.0, 0.1),
     'L1_conv_b_a_p': (0.0, 0.1),
     'L1_conv_b_a_g': (0.0, 0.341),
     'L1_conv_b_b_p': (0.0, 0.1),
     'L1_conv_b_b_g': (0.0, 0.361),
     'L1_conv_b_g': (0.0, 0.435),
     'L1_conv_ln_out_w': (1.0, 0.2),
     'L1_conv_ln_out_b': (0.0, 0.1),
     'L1_conv_b_o': (0.0, 0.1),
     'L2_conv_norm_a': (1.0, 0.2),
     'L2_conv_norm_b': (0.0, 0.1),
     'L2_conv_bl': (0.0, 0.1),
     'L2_conv_br': (0.0, 0.1),
     'L2_conv_blg': (1.0, 0.6),
     'L2_conv_brg': (1.0, 0.6),
     'L2_conv_bog': (1.0, 0.2),
     'L2_conv_on_a': (1.0, 0.2),
     'L2_conv_on_b': (0.0, 0.1),
     'L2_conv_bo': (0.0, 0.1),
     'L3_conv_ln_w': (1.0, 0.2),
     'L3_conv_ln_b': (0.0, 0.1)}
    factors = {}
    for name, (base, spread) in spreads.items():
        noise = np.random.default_rng([zlib.crc32(name.encode()), seed]).standard_normal(out[name].shape)
        drawn = base * np.exp(spread * noise) if base else spread * noise
        out[name] = jnp.asarray(drawn.astype(out[name].dtype))
    for name, factor in factors.items():
        out[name] = (out[name] * factor).astype(out[name].dtype)
    return out
```

```python
from contextlib import ExitStack

import concourse.bass as bass
from concourse import mybir

F32 = mybir.dt.float32
BF16 = mybir.dt.bfloat16
U8 = mybir.dt.uint8
ALU = mybir.AluOpType
ACT = mybir.ActivationFunctionType

P = 128
C = 64
N = 192
HALF = N // 2
ROWS = 2
TILE = ROWS * N
TILES = HALF // ROWS
TAIL = N - P
COLS = 3 * C
RING = 4
TURNS = TILES // RING
SUBS = ROWS * TILES
GROUP = 4
GROUPS = C // GROUP
CHUNKS = TILE // P
LAYERS = 4
GN_EPS = 1e-5
LN_EPS = 1e-5

LN_W, LN_B, GATE_B, LN2_W, LN2_B, OUT_B, NCOL = 0, 1, 2, 3, 4, 5, 6
K_CENTRE, K_GROUP, K_IDENT, K_SEL, K_PARITY, K_PART, NCONST = 0, 128, 256, 384, 386, 514, 517

HAS_LN = (True, True, True, False)
HAS_BIAS = (True, True, True, False)
HAS_MASK = (True, True, False, True)
GATE_FIRST = (True, False, True, False)
T_SCALE = (1.0, 1.0, 1.0 / N, 1.0)


def build_triangle_layers(nc, x_in, params, consts, mask3_k, mask3_row, x_out):
    scratch = nc.dram_tensor("x_scratch", [TILES, P, TILE], F32).ap()
    gate_dram = nc.dram_tensor("gate_scratch", [TILES, P, TILE], F32).ap()
    t_f32 = nc.dram_tensor("t_scratch", [C, N * N], F32).ap()
    t_bf16 = nc.dram_tensor("t_scratch_bf16", [C, N * N], BF16).ap()

    with ExitStack() as ctx:
        def sb(name, shape, dt=F32):
            return ctx.enter_context(nc.sbuf_tensor(name, shape, dt))

        def sem(name):
            return ctx.enter_context(nc.semaphore(name))

        def sems(name, n=RING):
            return [sem(f"{name}{i}") for i in range(n)]

        lr = sb("lr", [P, COLS * N])
        in_ring = sb("in_ring", [P, RING, TILE])
        res_ring = sb("res_ring", [P, RING, TILE])
        gate_ring = sb("gate_ring", [P, RING, TILE])
        new_ring = sb("new_ring", [P, RING, TILE])
        cen = sb("cen", [P, RING, TILE])
        sq = sb("sq", [P, 2, TILE])
        rb = sb("rb", [P, 2, TILE])
        xn = sb("xn", [P, 2, TILE])
        act_out = sb("act_out", [P, 2, TILE])
        val = sb("val", [P, 2, TILE])
        w_proj = sb("w_proj", [P, 512])
        w_bias = sb("w_bias", [P, 2 * COLS])
        w_gate = sb("w_gate", [P, P])
        w_out = sb("w_out", [P, P])
        w_out_s = sb("w_out_s", [P, 2, P])
        cols = sb("cols", [P, 2, NCOL])
        lnb6 = sb("lnb6", [P, 6])
        pb6 = sb("pb6", [6, 2 * COLS])
        bias_f = sb("bias_f", [6, 2, 2 * COLS])
        bias_part = sb("bias_part", [6, 2, 2 * COLS], BF16)
        bias_rows = sb("bias_rows", [6, 2 * COLS], BF16)
        gate_bias = sb("gate_bias", [P, 1])
        out_bias = sb("out_bias", [P, 2])
        mask = sb("mask", [P, 2, N])
        mask_k8 = sb("mask_k8", [P, 2], U8)
        mask_k = sb("mask_k", [P, 2])
        mask_row8 = sb("mask_row8", [P, N], U8)
        k = sb("k", [P, NCONST])
        centre_bf = sb("centre_bf", [P, P], BF16)
        parity_bf = sb("parity_bf", [6, P], BF16)
        w_centre = sb("w_centre", [P, P])
        half_col = sb("half_col", [P, 2 * CHUNKS])
        ve = sb("ve", [P, 2, 2 * CHUNKS])
        rstd = sb("rstd", [P, 2, 2 * CHUNKS])
        stats = sb("stats", [P, TILES, 6])
        mv = sb("mv", [P, 2])
        gn = sb("gn", [P, 8])
        ps = ctx.enter_context(nc.psum_tensor("ps", [P, 8, 512], F32))

        k_centre = k[:, K_CENTRE:K_CENTRE + P]
        k_group = k[:, K_GROUP:K_GROUP + P]
        k_ident = k[:, K_IDENT:K_IDENT + P]
        k_sel = k[:, K_SEL:K_SEL + 2]
        gn_mean, gn_dev, gn_q, gn_ve, gn_a, gn_b, gn_cb = (gn[:, i:i + 1] for i in range(7))

        in_loaded, res_loaded, gate_loaded = sems("in_loaded"), sems("res_loaded"), sems("gate_loaded")
        gate_stored, new_stored = sems("gate_stored"), sems("new_stored")
        planes_stored = sems("planes_stored", 2)
        consts_loaded, params_loaded, turned_stored = sem("consts_loaded"), sem("params_loaded"), sem("turned_stored")
        consts_ready, bias_mm, params_chain, params_ready = (
            sem("consts_ready"), sem("bias_mm"), sem("params_chain"), sem("params_ready"))
        mask_ready = sem("mask_ready")
        stats_done, gn_dve, gn_pe, gn_pool = sem("stats_done"), sem("gn_dve"), sem("gn_pe"), sem("gn_pool")
        a_z, a_cen, a_sq, a_var, a_ve, a_rstd, a_rb, a_bc, a_xn = (
            sem("a_" + s) for s in ("z", "cen", "sq", "var", "ve", "rstd", "rb", "bc", "xn"))
        a_gate_mm, a_gate, a_proj, a_sig, a_masked, a_free = (
            sem("a_" + s) for s in ("gate_mm", "gate", "proj", "sig", "masked", "free"))
        b1_mm, b1_main, b1_tail = sem("b1_mm"), sem("b1_main"), sem("b1_tail")
        b2_z, b2_cen, b2_sq, b2_var, b2_ve, b2_rstd, b2_rb, b2_bc, b2_zn = (
            sem("b2_" + s) for s in ("z", "cen", "sq", "var", "ve", "rstd", "rb", "bc", "zn"))
        b2_aff, b2_val, b2_out, b2_gated, b2_new, b2_stat, b2_turned = (
            sem("b2_" + s) for s in ("aff", "val", "out", "gated", "new", "stat", "turned"))

        def x_src(l):
            return x_in if l == 0 else scratch

        def x_dst(l):
            return x_out if l == LAYERS - 1 else scratch

        def lr_view(l):
            flat = lr[:, :].bitcast(BF16)[:, 0:COLS * N] if l == 0 else lr[:, :]
            return flat.rearrange("p (c r) -> p c r", r=N)

        turned = lr[:, 0:N * HALF].rearrange("p (j i) -> p j i", i=HALF)

        def t_dram(l):
            return t_bf16 if l == 0 else t_f32

        def t_tile(l, n):
            return t_dram(l).rearrange("c (h t f) -> h c t f", h=2, f=TILE)[:, :, n, :]

        def t_slot(l, s):
            return in_ring[:, s, :].bitcast(BF16)[:, 0:TILE] if l == 0 else in_ring[:, s, :]

        def plane_out(l, g):
            main = in_ring[:, 2 * g:2 * g + 2, :].rearrange("p a b -> p (a b)")
            tail = cen[:, g, :]
            if l == 0:
                main, tail = main.bitcast(BF16)[:, 0:GROUP * N], tail.bitcast(BF16)[:, 0:2 * N]
            return main.rearrange("p (d q) -> p d q", q=N), tail.rearrange("p (d q) -> p d q", q=N)

        def in_count(l, phase):
            turns = TURNS
            return 16 * turns * (1 + 3 * l + phase)

        n_params = [7 + (1 if l < 2 else (2 if HAS_MASK[l] else 0)) for l in range(LAYERS)]

        def params_count(l):
            return 16 * sum(n_params[:l + 1])

        def gated_before(l):
            return sum(TILES for m in range(l) if not GATE_FIRST[m])

        def val_before(l):
            return sum(TILES for m in range(l) if GATE_FIRST[m])

        def masked_before(l):
            return sum(SUBS for m in range(l) if HAS_MASK[m])

        def slot_free(eng, semaphore, value):
            if not (isinstance(value, int) and value <= 0):
                eng.wait_ge(semaphore, value)

        def over_tiles(eng, step):
            for s in range(RING):
                step(s, 0, s, RING)
            with eng.Fori(1, TURNS - 1) as i:
                for s in range(RING):
                    step(i * RING + s, i, s, RING)
            for s in range(RING):
                step(TILES - RING + s, TURNS - 1, s, RING - 1 - s)

        block = ctx.enter_context(nc.Block())

        @block.sync
        def _(sp):
            sp.dma_start(k[:, :], consts).then_inc(consts_loaded, 16)

            def load_params(l):
                pr = params[l]
                dst = [(w_proj, "w_proj"), (w_bias, "w_bias"), (w_gate, "w_gate"), (w_out, "w_out"),
                       (lnb6, "lnb6"), (pb6, "pb6")]
                for tile, name in dst:
                    sp.dma_start(tile[:, :], pr[name]).then_inc(params_loaded, 16)
                sp.dma_start(cols[:, l % 2, :], pr["cols"]).then_inc(params_loaded, 16)
                if "mask" in pr:
                    sp.dma_start(mask[:, :, :], pr["mask"]).then_inc(params_loaded, 16)
                elif HAS_MASK[l]:
                    sp.dma_start(mask_k8[:, :], mask3_k).then_inc(params_loaded, 16)
                    sp.dma_start(mask_row8[:, :], mask3_row).then_inc(params_loaded, 16)

            def load_x(n, i, s):
                sp.wait_ge(stats_done, n - RING + 1)
                sp.dma_start(in_ring[:, s, :], x_in[n, :, :]).then_inc(in_loaded[s], 16)

            def phase_a(l):
                src, used = x_src(l), (a_z if HAS_LN[l] else a_xn)
                for s in range(RING):
                    sp.dma_start(in_ring[:, s, :], src[s, :, :]).then_inc(in_loaded[s], 16)

                def step(n, i, s, ahead):
                    if ahead == RING:
                        sp.wait_ge(used, l * TILES + n + 1)
                        sp.dma_start(in_ring[:, s, :], src[n + RING, :, :]).then_inc(in_loaded[s], 16)
                    sp.wait_ge(a_gate, l * TILES + n + 1)
                    sp.dma_start(gate_dram[n, :, :], gate_ring[:, s, :]).then_inc(gate_stored[s], 16)

                over_tiles(sp, step)

            def phase_b1(l):
                dram = t_dram(l).rearrange("(g d) (i j) -> g i d j", d=GROUP, j=N)
                for g in range(GROUPS):
                    main, tail = plane_out(l, g % 2)
                    sp.wait_ge(b1_main, l * GROUPS + g + 1)
                    sp.dma_start(dram[g, 0:P, :, :], main).then_inc(planes_stored[g % 2], 16)
                    sp.wait_ge(b1_tail, l * GROUPS + g + 1)
                    for e in range(2):
                        sp.dma_start(dram[g, P:N, e::2, :], tail[TAIL * e:TAIL * e + TAIL, :, :])\
                            .then_inc(planes_stored[g % 2], 16)

            def phase_b2(l):
                src, dst = x_src(l), x_dst(l)
                for s in range(2):
                    sp.wait_ge(planes_stored[s], (l + 1) * 48 * (GROUPS // 2))
                for s in range(RING):
                    sp.wait_ge(gate_stored[s], (l + 1) * 16 * TURNS)

                def load_t(n, s):
                    for h in range(2):
                        sp.dma_start(t_slot(l, s)[C * h:C * h + C, :], t_tile(l, n)[h, :, :]).then_inc(in_loaded[s], 16)

                def load_late(n, s):
                    sp.dma_start(res_ring[:, s, :], src[n, :, :]).then_inc(res_loaded[s], 16)
                    sp.dma_start(gate_ring[:, s, :], gate_dram[n, :, :]).then_inc(gate_loaded[s], 16)

                for s in range(RING):
                    load_t(s, s)
                    load_late(s, s)

                def step(n, i, s, ahead):
                    if ahead == RING:
                        sp.wait_ge(b2_z, l * TILES + n + 1)
                        load_t(n + RING, s)
                    sp.wait_ge(b2_new, l * TILES + n + 1)
                    if l != 1:
                        sp.dma_start(dst[n, :, :], new_ring[:, s, :]).then_inc(new_stored[s], 16)
                    if ahead == RING:
                        load_late(n + RING, s)

                over_tiles(sp, step)
                if l == 1:
                    sp.wait_ge(b2_turned, TILES)
                    for h in range(2):
                        for h2 in range(2):
                            for r in range(ROWS):
                                s_ap = turned[C * h:C * h + C, h2 * HALF + r:(h2 + 1) * HALF:ROWS, :]
                                d_ap = scratch.rearrange("t (h c) (r h2 i) -> h h2 r c t i", h=2, r=ROWS, h2=2)
                                sp.dma_start(d_ap[h2, h, r, :, :, :], s_ap).then_inc(turned_stored, 16)
                    sp.wait_ge(turned_stored, 16 * 8)
                else:
                    stores = sum(1 for m in range(l + 1) if m != 1)
                    for s in range(RING):
                        sp.wait_ge(new_stored[s], stores * 16 * TURNS)

            load_params(0)
            for s in range(RING):
                sp.dma_start(in_ring[:, s, :], x_in[s, :, :]).then_inc(in_loaded[s], 16)
            with sp.Fori(1, TURNS) as i:
                for s in range(RING):
                    load_x(i * RING + s, i, s)
            sp.wait_ge(stats_done, TILES)
            for l in range(LAYERS):
                phase_a(l)
                sp.wait_ge(a_free, (l + 1) * SUBS + 2)
                if l + 1 < LAYERS:
                    load_params(l + 1)
                phase_b1(l)
                phase_b2(l)

        @block.tensor
        def _(pe):
            def params_biases(l):
                pe.wait_ge(params_loaded, params_count(l))
                nc.tensor.matmul(ps[0:6, 7, 0:2 * COLS], lnb6[:, :], w_bias[:, :], start=True, stop=True)
                nc.tensor.matmul(ps[:, 7, 400:401], w_gate[:, :], cols[:, l % 2, LN_B:LN_B + 1], start=True, stop=True)
                nc.tensor.matmul(ps[:, 7, 402:403], w_out[:, :], cols[:, l % 2, LN2_B:LN2_B + 1],
                                 start=True, stop=True).then_inc(bias_mm, 1)

            def group_norm(l):
                pe.wait_ge(gn_dve, 7 * l + 1)
                nc.tensor.matmul(ps[:, 6, 0:1], k_group, mv[:, 0:1], start=True, stop=True).then_inc(gn_pe, 1)
                pe.wait_ge(gn_dve, 7 * l + 4)
                nc.tensor.matmul(ps[:, 6, 2:3], k_group, gn_q, start=True, stop=True).then_inc(gn_pe, 1)
                pe.wait_ge(gn_dve, 7 * l + 6)
                nc.tensor.matmul(ps[:, 6, 4:5], k_centre, gn_b, start=True, stop=True).then_inc(gn_pe, 1)

            def phase_a(l):
                base = l * TILES
                ln = HAS_LN[l]
                pe.wait_ge(gn_dve, 7 * (l + 1))
                pe.wait_ge(params_ready, l + 1)

                def centre(n, i, s):
                    pe.wait_ge(in_loaded[s], in_count(l, 0) + 16 * (i + 1))
                    slot_free(pe, a_sq, base + n - 1)
                    nc.tensor.matmul(ps[:, s % 2, 0:TILE], w_centre[:, :], in_ring[:, s, :],
                                     start=True, stop=True).then_inc(a_z, 1)

                def variance(n, s):
                    pe.wait_ge(a_sq, base + n + 1)
                    slot_free(pe, a_xn, base + n)
                    for j in range(CHUNKS):
                        mm = nc.tensor.matmul(ps[:, 2, TILE + 2 * j:TILE + 2 * j + 2],
                                              sq[:, s % 2, P * j:P * j + P], k_sel, start=True, stop=True)
                    mm.then_inc(a_var, 1)

                def spread(n, s):
                    pe.wait_ge(a_rb, base + n + 1)
                    for j in range(CHUNKS):
                        mm = nc.tensor.transpose(ps[:, 2, P * j:P * j + P], rb[:, s % 2, P * j:P * j + P], k_ident)
                    mm.then_inc(a_bc, 1)

                def gate(n, s):
                    pe.wait_ge(a_xn, base + n + 1)
                    slot_free(pe, a_gate, base + n)
                    nc.tensor.matmul(ps[:, 3, 0:TILE], w_gate[:, :], xn[:, s % 2, :],
                                     start=True, stop=True).then_inc(a_gate_mm, 1)

                def project(n, s, r):
                    m = ROWS * n + r
                    pe.wait_ge(a_free, l * SUBS + m + 1)
                    first = not HAS_BIAS[l]
                    if HAS_BIAS[l]:
                        for h in range(2):
                            nc.tensor.matmul(ps[:, 4 + 2 * r + h, 0:2 * COLS], parity_bf[:, :], bias_rows[:, :],
                                             start=True, stop=False, skip_group_check=True)
                    for h in range(2):
                        bank = ps[:, 4 + 2 * r + h, 0:2 * COLS].rearrange("p (v c) -> p v c", v=2)
                        nc.tensor.matmul(bank[:, :, 0:P], xn[C * h:C * h + C, s % 2, N * r:N * r + P],
                                         w_proj[C * h:C * h + C, 0:2 * P], start=first, stop=True,
                                         skip_group_check=True)
                    for e in range(2):
                        for h in range(2):
                            bank = ps[:, 4 + 2 * r + h, 0:2 * COLS].rearrange("p (v c) -> p v c", v=2)
                            mm = nc.tensor.matmul(bank[TAIL * e:TAIL * e + TAIL, :, P:COLS],
                                                  xn[C * h:C * h + C, s % 2, N * r + P:N * r + N],
                                                  w_proj[C * h:C * h + C, 2 * P + P * e:3 * P + P * e],
                                                  start=first, stop=True, skip_group_check=True)
                    mm.then_inc(a_proj, 1)

                def step(n, i, s, ahead):
                    if ln and ahead >= 1:
                        variance(n + 1, (s + 1) % RING)
                    gate(n, s)
                    project(n, s, 0)
                    if ln and ahead >= 2:
                        centre(n + 2, i + (s + 2) // RING, (s + 2) % RING)
                    if ln and ahead >= 1:
                        spread(n + 1, (s + 1) % RING)
                    project(n, s, 1)

                if ln:
                    centre(0, 0, 0)
                    centre(1, 0, 1)
                    variance(0, 0)
                    spread(0, 0)
                over_tiles(pe, step)

            def phase_b1(l):
                v = lr_view(l)
                pe.wait_ge(a_free, (l + 1) * SUBS + 2)

                def main_lr(d):
                    return v[:, d, :], v[:, C + d, :]

                def tail_lr(d):
                    e = d % 2
                    return (v[TAIL * e:TAIL * e + TAIL, 2 * C + d // 2, :],
                            v[TAIL * e:TAIL * e + TAIL, 2 * C + C // 2 + d // 2, :])

                for g in range(GROUPS):
                    b = 3 * (g % 2)
                    if g >= 2:
                        pe.wait_ge(b1_main, l * GROUPS + g - 1)
                        pe.wait_ge(b1_tail, l * GROUPS + g - 1)
                    for pair in range(2):
                        even, odd = GROUP * g + 2 * pair, GROUP * g + 2 * pair + 1
                        q = slice(N * pair, N * pair + N)
                        for part, (lo, hi) in ((main_lr, (True, False)), (tail_lr, (False, True))):
                            for e, d in enumerate((even, odd)):
                                left, right = part(d)
                                nc.tensor.matmul(ps[:, b + e, q], left[:, 0:P], right, start=lo, stop=hi)
                        for part, d, lo in ((tail_lr, even, True), (main_lr, odd, True),
                                            (main_lr, even, False), (tail_lr, odd, False)):
                            e = d % 2
                            left, right = part(d)
                            mm = nc.tensor.matmul(ps[TAIL * e:TAIL * e + TAIL, b + 2, q], left[:, P:N], right,
                                                  start=lo, stop=not lo, skip_group_check=True)
                    mm.then_inc(b1_mm, 1)

            def phase_b2(l):
                base = l * TILES
                w_c = centre_bf[:, :] if l == 0 else k_centre

                def centre(n, i, s):
                    pe.wait_ge(in_loaded[s], in_count(l, 1) + 32 * (i + 1))
                    slot_free(pe, b2_sq, base + n - 1)
                    nc.tensor.matmul(ps[:, s % 2, 0:TILE], w_c, t_slot(l, s), start=True, stop=True).then_inc(b2_z, 1)

                def variance(n, s):
                    pe.wait_ge(b2_sq, base + n + 1)
                    slot_free(pe, b2_zn, base + n - 1)
                    for j in range(CHUNKS):
                        mm = nc.tensor.matmul(ps[:, 2 + s % 2, TILE + 2 * j:TILE + 2 * j + 2],
                                              sq[:, s % 2, P * j:P * j + P], k_sel, start=True, stop=True)
                    mm.then_inc(b2_var, 1)

                def spread(n, s):
                    pe.wait_ge(b2_rb, base + n + 1)
                    for j in range(CHUNKS):
                        mm = nc.tensor.transpose(ps[:, 2 + s % 2, P * j:P * j + P], rb[:, s % 2, P * j:P * j + P],
                                                 k_ident)
                    mm.then_inc(b2_bc, 1)

                def out(n, s):
                    if GATE_FIRST[l]:
                        pe.wait_ge(b2_val, val_before(l) + n + 1)
                    else:
                        pe.wait_ge(b2_zn, base + n + 1)
                    if GATE_FIRST[l]:
                        slot_free(pe, b2_new, base + n - 1)
                    else:
                        slot_free(pe, b2_gated, gated_before(l) + n - 1)
                    nc.tensor.matmul(ps[:, 4 + s % 2, 0:TILE], w_out_s[:, l % 2, :],
                                     (val if GATE_FIRST[l] else xn)[:, s % 2, :], start=True, stop=True)\
                        .then_inc(b2_out, 1)

                def step(n, i, s, ahead):
                    if ahead >= 3:
                        centre(n + 3, i + (s + 3) // RING, (s + 3) % RING)
                    if ahead >= 2:
                        variance(n + 2, (s + 2) % RING)
                    if ahead >= 1:
                        spread(n + 1, (s + 1) % RING)
                    out(n, s)

                for n in range(3):
                    centre(n, 0, n)
                for n in range(2):
                    variance(n, n)
                spread(0, 0)
                over_tiles(pe, step)

            pe.wait_ge(consts_ready, 1)
            params_biases(0)
            group_norm(0)
            for l in range(LAYERS):
                phase_a(l)
                phase_b1(l)
                if l + 1 < LAYERS:
                    params_biases(l + 1)
                phase_b2(l)
                if l + 1 < LAYERS:
                    group_norm(l + 1)

        @block.scalar
        def _(act):
            def phase_a(l):
                base = l * TILES
                ln = HAS_LN[l]
                act.wait_ge(gn_dve, 7 * (l + 1))
                act.wait_ge(params_ready, l + 1)

                def centred(n, s):
                    act.wait_ge(a_z, base + n + 1)
                    slot_free(act, a_xn, base + n - 1)
                    slot_free(act, a_var, base + n - 1)
                    nc.scalar.activation(cen[:, s, :], ps[:, s % 2, 0:TILE], ACT.Identity, bias=gn_cb)\
                        .then_inc(a_cen, 1)
                    nc.scalar.activation(sq[:, s % 2, :], ps[:, s % 2, 0:TILE], ACT.Square, bias=gn_cb)\
                        .then_inc(a_sq, 1)

                def spread(n, s):
                    act.wait_ge(a_rstd, base + n + 1)
                    slot_free(act, a_bc, base + n - 1)
                    nc.scalar.activation(rb[:, s % 2, :].rearrange("p (a c) -> p a c", c=C),
                                         rstd[:, s % 2, :].rearrange("p (a o) -> p a o", o=1)
                                         .broadcast_to([P, 2 * CHUNKS, C]), ACT.Copy).then_inc(a_rb, 1)

                def plain(n, i, s):
                    act.wait_ge(in_loaded[s], in_count(l, 0) + 16 * (i + 1))
                    slot_free(act, a_proj, l * SUBS + ROWS * (n - 1))
                    slot_free(act, a_gate_mm, base + n - 1)
                    nc.scalar.activation(xn[:, s % 2, :], in_ring[:, s, :], ACT.Identity, bias=gn_b, scale=gn_a)\
                        .then_inc(a_xn, 1)

                def gate(n, i, s):
                    act.wait_ge(a_gate_mm, base + n + 1)
                    slot_free(act, gate_stored[s], 16 * (l * TURNS + i))
                    nc.scalar.activation(gate_ring[:, s, :], ps[:, 3, 0:TILE], ACT.Sigmoid, bias=gate_bias[:, 0:1])\
                        .then_inc(a_gate, 1)

                def sigmoids(n, s, r):
                    m = ROWS * n + r
                    act.wait_ge(a_proj, l * SUBS + m + 1)
                    act.wait_ge(a_free, l * SUBS + m + 1)
                    nc.scalar.activation(act_out[:, r, :].rearrange("p (h c) -> p h c", h=2),
                                         ps[:, 4 + 2 * r:6 + 2 * r, COLS:2 * COLS], ACT.Sigmoid).then_inc(a_sig, 1)

                def step(n, i, s, ahead):
                    gate(n, i, s)
                    if ln and ahead >= 1:
                        spread(n + 1, (s + 1) % RING)
                    sigmoids(n, s, 0)
                    if ln and ahead >= 2:
                        centred(n + 2, (s + 2) % RING)
                    if not ln and ahead >= 1:
                        plain(n + 1, i + (s + 1) // RING, (s + 1) % RING)
                    sigmoids(n, s, 1)

                if ln:
                    centred(0, 0)
                    centred(1, 1)
                    spread(0, 0)
                else:
                    plain(0, 0, 0)
                over_tiles(act, step)

            def phase_b1(l):
                for g in range(GROUPS):
                    main, _ = plane_out(l, g % 2)
                    act.wait_ge(b1_mm, l * GROUPS + g + 1)
                    if g >= 2:
                        act.wait_ge(planes_stored[g % 2], 48 * (l * (GROUPS // 2) + g // 2))
                    b = 3 * (g % 2)
                    nc.scalar.activation(main.rearrange("p (a e) q -> p e a q", e=2),
                                         ps[:, b:b + 2, 0:2 * N].rearrange("p e (a q) -> p e a q", q=N),
                                         ACT.Copy).then_inc(b1_main, 1)

            def phase_b2(l):
                base = l * TILES

                def centred(n, s):
                    act.wait_ge(b2_z, base + n + 1)
                    slot_free(act, b2_zn, base + n - RING + 1)
                    slot_free(act, b2_var, base + n - 1)
                    nc.scalar.activation(cen[:, s, :], ps[:, s % 2, 0:TILE], ACT.Copy, scale=T_SCALE[l])\
                        .then_inc(b2_cen, 1)
                    nc.scalar.activation(sq[:, s % 2, :], ps[:, s % 2, 0:TILE], ACT.Square, scale=T_SCALE[l])\
                        .then_inc(b2_sq, 1)

                def spread(n, s):
                    act.wait_ge(b2_rstd, base + n + 1)
                    slot_free(act, b2_bc, base + n - 1)
                    nc.scalar.activation(rb[:, s % 2, :].rearrange("p (a c) -> p a c", c=C),
                                         rstd[:, s % 2, :].rearrange("p (a o) -> p a o", o=1)
                                         .broadcast_to([P, 2 * CHUNKS, C]), ACT.Copy).then_inc(b2_rb, 1)

                def affine(n, s):
                    act.wait_ge(b2_zn, base + n + 1)
                    slot_free(act, b2_val, val_before(l) + n - 1)
                    nc.scalar.activation(act_out[:, s % 2, :], xn[:, s % 2, :], ACT.Identity,
                                         bias=cols[:, l % 2, LN2_B:LN2_B + 1],
                                         scale=cols[:, l % 2, LN2_W:LN2_W + 1]).then_inc(b2_aff, 1)

                def step(n, i, s, ahead):
                    if ahead >= 3:
                        centred(n + 3, (s + 3) % RING)
                    if ahead >= 2:
                        spread(n + 2, (s + 2) % RING)
                    if GATE_FIRST[l] and ahead >= 1:
                        affine(n + 1, (s + 1) % RING)
                    if l == 1:
                        act.wait_ge(b2_new, base + n + 1)
                        nc.scalar.activation(turned[:, :, bass.ds(ROWS * n, ROWS)].rearrange("p j i -> p i j"),
                                             new_ring[:, s, :].rearrange("p (r j) -> p r j", r=ROWS),
                                             ACT.Copy).then_inc(b2_turned, 1)

                for n in range(3):
                    centred(n, n)
                for n in range(2):
                    spread(n, n)
                if GATE_FIRST[l]:
                    affine(0, 0)
                over_tiles(act, step)

            for l in range(LAYERS):
                phase_a(l)
                phase_b1(l)
                phase_b2(l)

        @block.vector
        def _(dve):
            dve.sem_inc(a_free, 2)
            dve.wait_ge(consts_loaded, 16)
            nc.vector.tensor_copy(centre_bf[:, :], k_centre)
            nc.vector.tensor_copy(parity_bf[:, :], k[0:6, K_PARITY:K_PARITY + P]).then_inc(consts_ready, 1)

            def params_scaled(l):
                c = cols[:, l % 2, :]
                chain = [8 * l]

                def link(ins):
                    chain[0] += 1
                    ins.then_inc(params_chain, 1)
                    dve.wait_ge(params_chain, chain[0])

                dve.wait_ge(params_loaded, params_count(l))
                dve.wait_ge(bias_mm, l + 1)
                link(nc.vector.tensor_tensor(bias_f[:, 0, :], ps[0:6, 7, 0:2 * COLS], pb6[:, :], ALU.add))
                link(nc.vector.tensor_copy(bias_part[:, 0, :], bias_f[:, 0, :]))
                link(nc.vector.tensor_tensor(bias_f[:, 1, :], bias_f[:, 0, :], bias_part[:, 0, :], ALU.subtract))
                link(nc.vector.tensor_copy(bias_part[:, 1, :], bias_f[:, 1, :]))
                link(nc.vector.tensor_tensor(bias_f[:, 0, :], bias_f[:, 1, :], bias_part[:, 1, :], ALU.subtract))
                link(nc.vector.tensor_scalar(bias_rows[:, :], bias_f[:, 0, :], k[0:6, K_PART + 2:K_PART + 3], None, ALU.mult))
                link(nc.vector.scalar_tensor_tensor(bias_rows[:, :], bias_part[:, 0, :], k[0:6, K_PART:K_PART + 1],
                                                    bias_rows[:, :], ALU.mult, ALU.add))
                link(nc.vector.scalar_tensor_tensor(bias_rows[:, :], bias_part[:, 1, :], k[0:6, K_PART + 1:K_PART + 2],
                                                    bias_rows[:, :], ALU.mult, ALU.add))
                nc.vector.tensor_tensor(gate_bias[:, :], ps[:, 7, 400:401], c[:, GATE_B:GATE_B + 1], ALU.add)
                nc.vector.tensor_scalar(w_proj[:, :], w_proj[:, :], c[:, LN_W:LN_W + 1], None, ALU.mult)
                nc.vector.tensor_scalar(w_gate[:, :], w_gate[:, :], c[:, LN_W:LN_W + 1], None, ALU.mult)
                if HAS_MASK[l] and l >= 2:
                    nc.vector.tensor_copy(mask_k[:, :], mask_k8[:, :]).then_inc(mask_ready, 1)
                    dve.wait_ge(mask_ready, 1)
                    for t in range(2):
                        nc.vector.tensor_scalar(mask[:, t, :], mask_row8[:, :], mask_k[:, t:t + 1], None, ALU.mult)
                if GATE_FIRST[l]:
                    nc.vector.tensor_copy(out_bias[:, l % 2:l % 2 + 1], c[:, OUT_B:OUT_B + 1])
                    nc.vector.tensor_copy(w_out_s[:, l % 2, :], w_out[:, :]).then_inc(params_ready, 1)
                else:
                    nc.vector.tensor_tensor(out_bias[:, l % 2:l % 2 + 1], ps[:, 7, 402:403], c[:, OUT_B:OUT_B + 1], ALU.add)
                    nc.vector.tensor_scalar(w_out_s[:, l % 2, :], w_out[:, :], c[:, LN2_W:LN2_W + 1], None,
                                            ALU.mult).then_inc(params_ready, 1)

            def group_norm(l):
                b = 7 * l
                dve.wait_ge(stats_done, (l + 1) * TILES)
                nc.vector.bn_aggr(mv[:, :], stats[:, :, :].rearrange("p t s -> p (t s)")).then_inc(gn_dve, 1)
                dve.wait_ge(gn_pe, 3 * l + 1)
                nc.vector.tensor_copy(gn_mean, ps[:, 6, 0:1]).then_inc(gn_dve, 1)
                dve.wait_ge(gn_dve, b + 2)
                nc.vector.tensor_tensor(gn_dev, mv[:, 0:1], gn_mean, ALU.subtract).then_inc(gn_dve, 1)
                dve.wait_ge(gn_dve, b + 3)
                nc.vector.scalar_tensor_tensor(gn_q, gn_dev, gn_dev, mv[:, 1:2], ALU.mult, ALU.add).then_inc(gn_dve, 1)
                dve.wait_ge(gn_pe, 3 * l + 2)
                nc.vector.tensor_scalar(gn_ve, ps[:, 6, 2:3], GN_EPS, None, ALU.add).then_inc(gn_dve, 1)
                dve.wait_ge(gn_pool, l + 1)
                nc.vector.tensor_scalar(gn_b, gn_mean, gn_a, -1.0, ALU.mult, ALU.mult).then_inc(gn_dve, 1)
                nc.vector.tensor_scalar(w_centre[:, :], k_centre, gn_a, None, ALU.mult)
                dve.wait_ge(gn_pe, 3 * l + 3)
                nc.vector.tensor_copy(gn_cb, ps[:, 6, 4:5]).then_inc(gn_dve, 1)

            def phase_a(l):
                base = l * TILES
                ln = HAS_LN[l]
                out4 = lr_view(l).rearrange("p c (h r) -> p h c r", h=2)
                if l:
                    dve.wait_ge(b1_mm, l * GROUPS)
                if l == 2:
                    dve.wait_ge(turned_stored, 16 * 8)

                def var_eps(n, s):
                    dve.wait_ge(a_var, base + n + 1)
                    slot_free(dve, a_rstd, base + n - 1)
                    nc.vector.tensor_scalar(ve[:, s % 2, :], ps[:, 2, TILE:TILE + 2 * CHUNKS], LN_EPS, None,
                                            ALU.add).then_inc(a_ve, 1)

                def normalise(n, s):
                    dve.wait_ge(a_bc, base + n + 1)
                    dve.wait_ge(a_cen, base + n + 1)
                    slot_free(dve, a_proj, l * SUBS + ROWS * (n - 1))
                    nc.vector.tensor_tensor(xn[:, s % 2, :], ps[:, 2, 0:TILE], cen[:, s, :], ALU.mult)\
                        .then_inc(a_xn, 1)

                def glu(n, r):
                    m = ROWS * n + r
                    if HAS_MASK[l]:
                        dve.wait_ge(a_masked, masked_before(l) + m + 1)
                    else:
                        dve.wait_ge(a_sig, l * SUBS + m + 1)
                    nc.vector.tensor_tensor(out4[:, :, :, m], ps[:, 4 + 2 * r:6 + 2 * r, 0:COLS],
                                            act_out[:, r, :].rearrange("p (h c) -> p h c", h=2),
                                            ALU.mult).then_inc(a_free, 1)

                def step(n, i, s, ahead):
                    if ln and ahead >= 1:
                        var_eps(n + 1, (s + 1) % RING)
                    glu(n, 0)
                    if ln and ahead >= 1:
                        normalise(n + 1, (s + 1) % RING)
                    glu(n, 1)

                if ln:
                    var_eps(0, 0)
                    normalise(0, 0)
                over_tiles(dve, step)

            def phase_b1(l):
                for g in range(GROUPS):
                    _, tail = plane_out(l, g % 2)
                    dve.wait_ge(b1_mm, l * GROUPS + g + 1)
                    if g >= 2:
                        dve.wait_ge(planes_stored[g % 2], 48 * (l * (GROUPS // 2) + g // 2))
                    nc.vector.tensor_copy(tail, ps[:, 3 * (g % 2) + 2, 0:2 * N].rearrange("p (a q) -> p a q", q=N))\
                        .then_inc(b1_tail, 1)

            def phase_b2(l):
                base = l * TILES

                def var_eps(n, s):
                    dve.wait_ge(b2_var, base + n + 1)
                    slot_free(dve, b2_rstd, base + n - 1)
                    nc.vector.tensor_scalar(ve[:, s % 2, :], ps[:, 2 + s % 2, TILE:TILE + 2 * CHUNKS], LN_EPS, None,
                                            ALU.add).then_inc(b2_ve, 1)

                def normalise(n, s):
                    dve.wait_ge(b2_bc, base + n + 1)
                    dve.wait_ge(b2_cen, base + n + 1)
                    if GATE_FIRST[l]:
                        slot_free(dve, b2_aff, val_before(l) + n - 1)
                    else:
                        slot_free(dve, b2_out, base + n - 1)
                    nc.vector.tensor_tensor(xn[:, s % 2, :], ps[:, 2 + s % 2, 0:TILE], cen[:, s, :], ALU.mult)\
                        .then_inc(b2_zn, 1)

                def finish(n, i, s):
                    bias = out_bias[:, l % 2:l % 2 + 1]
                    dve.wait_ge(b2_out, base + n + 1)
                    if GATE_FIRST[l]:
                        dve.wait_ge(res_loaded[s], 16 * (l * TURNS + i + 1))
                        slot_free(dve, new_stored[s], 16 * (l // 2 * TURNS + i))
                        nc.vector.scalar_tensor_tensor(new_ring[:, s, :], ps[:, 4 + s % 2, 0:TILE], bias,
                                                       res_ring[:, s, :], ALU.add, ALU.add).then_inc(b2_new, 1)
                    else:
                        dve.wait_ge(gate_loaded[s], 16 * (l * TURNS + i + 1))
                        slot_free(dve, b2_new, base + n - 1)
                        nc.vector.scalar_tensor_tensor(val[:, s % 2, :], ps[:, 4 + s % 2, 0:TILE], bias,
                                                       gate_ring[:, s, :], ALU.add, ALU.mult).then_inc(b2_gated, 1)

                def statistics(n, s):
                    dve.wait_ge(b2_new, base + n + 1)
                    nc.vector.bn_stats(stats[:, n, :], new_ring[:, s, :]).then_inc(stats_done, 1)

                def step(n, i, s, ahead):
                    if ahead >= 2:
                        var_eps(n + 2, (s + 2) % RING)
                    if ahead >= 1:
                        normalise(n + 1, (s + 1) % RING)
                    if not (isinstance(n, int) and n == 0) and l + 1 < LAYERS:
                        statistics(n - 1, (s - 1) % RING)
                    finish(n, i, s)

                var_eps(0, 0)
                var_eps(1, 1)
                normalise(0, 0)
                over_tiles(dve, step)
                if l + 1 < LAYERS:
                    statistics(TILES - 1, RING - 1)

            def first_statistics(i, s):
                dve.wait_ge(in_loaded[s], 16 * (i + 1))
                nc.vector.bn_stats(stats[:, i * RING + s, :], in_ring[:, s, :]).then_inc(stats_done, 1)

            params_scaled(0)
            with dve.Fori(0, TURNS) as i:
                for s in range(RING):
                    first_statistics(i, s)
            group_norm(0)
            for l in range(LAYERS):
                phase_a(l)
                phase_b1(l)
                if l + 1 < LAYERS:
                    params_scaled(l + 1)
                phase_b2(l)
                if l + 1 < LAYERS:
                    group_norm(l + 1)

        @block.gpsimd
        def _(pool):
            half_set = sem("half_set")
            nc.gpsimd.memset(half_col[:, :], -0.5).then_inc(half_set, 1)
            pool.wait_ge(half_set, 1)

            def group_norm(l):
                pool.wait_ge(gn_dve, 7 * l + 5)
                nc.gpsimd.tensor_tensor(gn_a, gn_ve, half_col[:, 0:1], ALU.pow).then_inc(gn_pool, 1)

            def phase_a(l):
                base = l * TILES
                ln = HAS_LN[l]
                mask4 = mask[:, :, :].rearrange("p t (h r) -> p t h r", h=2)
                pool.wait_ge(params_ready, l + 1)

                def inverse(n, s):
                    pool.wait_ge(a_ve, base + n + 1)
                    slot_free(pool, a_rb, base + n - 1)
                    nc.gpsimd.tensor_tensor(rstd[:, s % 2, :], ve[:, s % 2, :], half_col[:, :], ALU.pow)\
                        .then_inc(a_rstd, 1)

                def masked(n, r):
                    m = ROWS * n + r
                    pool.wait_ge(a_sig, l * SUBS + m + 1)
                    sig = act_out[:, r, :].rearrange("p (h c) -> p h c", h=2)
                    for t, (lo, hi) in enumerate(((0, P), (P, COLS))):
                        row = mask4[:, t, :, m].rearrange("p (h o) -> p h o", o=1).broadcast_to([P, 2, hi - lo])
                        ins = nc.gpsimd.tensor_tensor(sig[:, :, lo:hi], sig[:, :, lo:hi], row, ALU.mult)
                    ins.then_inc(a_masked, 1)

                def step(n, i, s, ahead):
                    if ln and ahead >= 1:
                        inverse(n + 1, (s + 1) % RING)
                    if HAS_MASK[l]:
                        masked(n, 0)
                        masked(n, 1)

                if ln:
                    inverse(0, 0)
                over_tiles(pool, step)

            def phase_b2(l):
                base = l * TILES

                def inverse(n, s):
                    pool.wait_ge(b2_ve, base + n + 1)
                    slot_free(pool, b2_rb, base + n - 1)
                    nc.gpsimd.tensor_tensor(rstd[:, s % 2, :], ve[:, s % 2, :], half_col[:, :], ALU.pow)\
                        .then_inc(b2_rstd, 1)

                def gated(n, i, s):
                    pool.wait_ge(b2_aff, val_before(l) + n + 1)
                    pool.wait_ge(gate_loaded[s], 16 * (l * TURNS + i + 1))
                    slot_free(pool, b2_out, base + n - 1)
                    nc.gpsimd.tensor_tensor(val[:, s % 2, :], act_out[:, s % 2, :], gate_ring[:, s, :], ALU.mult)\
                        .then_inc(b2_val, 1)

                def residual(n, i, s):
                    pool.wait_ge(b2_gated, gated_before(l) + n + 1)
                    pool.wait_ge(res_loaded[s], 16 * (l * TURNS + i + 1))
                    if l == 1:
                        slot_free(pool, b2_turned, n - RING + 1)
                        slot_free(pool, stats_done, (l + 1) * TILES + n - RING + 1)
                    else:
                        pool.wait_ge(new_stored[s], 16 * (2 * TURNS + i))
                    nc.gpsimd.tensor_tensor(new_ring[:, s, :], val[:, s % 2, :], res_ring[:, s, :], ALU.add)\
                        .then_inc(b2_new, 1)

                def step(n, i, s, ahead):
                    if ahead >= 2:
                        inverse(n + 2, (s + 2) % RING)
                    if GATE_FIRST[l]:
                        if ahead >= 1:
                            gated(n + 1, i + (s + 1) // RING, (s + 1) % RING)
                    else:
                        residual(n, i, s)

                inverse(0, 0)
                inverse(1, 1)
                if GATE_FIRST[l]:
                    gated(0, 0, 0)
                over_tiles(pool, step)

            group_norm(0)
            for l in range(LAYERS):
                phase_a(l)
                phase_b2(l)
                if l + 1 < LAYERS:
                    group_norm(l + 1)


def shape_constants():
    import numpy as np
    k = np.zeros((P, NCONST), np.float32)
    part = np.arange(P)
    same_half = part[:, None] // C == part[None, :] // C
    k[:, K_CENTRE:K_CENTRE + P] = np.eye(P) - same_half / C
    k[:, K_GROUP:K_GROUP + P] = (part[:, None] % C // 2 == part[None, :] % C // 2) / 4
    k[:, K_IDENT:K_IDENT + P] = np.eye(P)
    for h in range(2):
        k[C * h:C * h + C, K_SEL + h] = 1 / C
        k[3 * h:3 * h + 3, K_PARITY + TAIL * h:K_PARITY + TAIL * h + TAIL] = 1
    for r in range(6):
        k[r, K_PART + r % 3] = 1
    return k


def kernel(**inputs):
    import numpy as np
    import concourse.bacc as bacc
    from concourse.bass_utils import run_bass_kernel_spmd

    get = {name: np.asarray(a) for name, a in inputs.items()}

    def to_tiles(x):
        return np.ascontiguousarray(x.reshape(2, TILES, ROWS, N, C).transpose(1, 0, 4, 2, 3)).reshape(TILES, P, TILE)

    def blocks(w):
        out = np.zeros((P, P), np.float32)
        out[:C, :C] = w
        out[C:, C:] = w
        return out

    def params(l, left, right, left_g, right_g, gate, out, bias, ln, ln2, gate_b, out_b):
        values, gates = np.concatenate([left, right], 1), np.concatenate([left_g, right_g], 1)
        tails = [[np.concatenate([a[..., e::2], b[..., e::2]], -1) for a, b in ((left, right), (left_g, right_g))]
                 for e in range(2)]
        proj = np.concatenate([values, gates] + tails[0] + tails[1], 1)
        row = [np.concatenate([values, tails[e][0], gates, tails[e][1]], 1) for e in range(2)]
        bl, br, blg, brg = bias
        b_main = [np.concatenate([bl, br]), np.concatenate([blg, brg])]
        b_rows = [np.concatenate([b_main[0], bl[e::2], br[e::2], b_main[1], blg[e::2], brg[e::2]]) for e in range(2)]
        ln_w, ln_b = ln
        lnb6 = np.zeros((P, 6), np.float32)
        lnb6[:C, 0:3] = ln_b[:, None]
        lnb6[C:, 3:6] = ln_b[:, None]
        columns = np.stack([ln_w, ln_b, gate_b, ln2[0], ln2[1], out_b], 1)
        return {"w_proj": np.concatenate([proj, proj], 0), "w_bias": np.concatenate(row, 0),
                "w_gate": blocks(gate), "w_out": blocks(out), "lnb6": lnb6,
                "pb6": np.stack([b_rows[0]] * 3 + [b_rows[1]] * 3),
                "cols": np.concatenate([columns, columns], 0)}

    def mask_tiles(m):
        mt = m.reshape(N, N).T
        return np.stack([mt[:P], np.concatenate([mt[P:], mt[P:]], 0)], 1)

    zero, one = np.zeros(C, np.float32), np.ones(C, np.float32)
    a, b, c, d = ({n[8:]: v for n, v in get.items() if n.startswith(f"L{l}_conv_")} for l in range(LAYERS))
    layers = [
        params(0, a["Wl"].T, a["Wr"].T, a["Wlg"].T, a["Wrg"].T, a["Wog"].T, a["Wout"].T, (zero,) * 4,
               (a["ln1_w"], a["ln1_b"]), (a["ln2_w"], a["ln2_b"]), zero, zero),
        params(1, b["w_a_p"], b["w_b_p"], b["w_a_g"], b["w_b_g"], b["w_g"], b["w_o"],
               (b["b_a_p"], b["b_b_p"], b["b_a_g"], b["b_b_g"]),
               (b["ln_in_w"], b["ln_in_b"]), (b["ln_out_w"], b["ln_out_b"]), b["b_g"], b["b_o"]),
        params(2, c["Wl"], c["Wr"], c["Wlg"], c["Wrg"], c["Wog"], c["Wo"],
               (c["bl"], c["br"], c["blg"], c["brg"]),
               (c["norm_a"], c["norm_b"]), (c["on_a"], c["on_b"]), c["bog"], c["bo"]),
        params(3, d["W_lr"][:, 0:C], d["W_lr"][:, C:2 * C], d["W_lr"][:, 2 * C:3 * C], d["W_lr"][:, 3 * C:4 * C],
               d["W_gate"], d["W_out"], (zero,) * 4, (one, zero), (d["ln_w"], d["ln_b"]), zero, zero),
    ]
    layers[0]["mask"] = mask_tiles(a["mask"])
    layers[1]["mask"] = mask_tiles(b["mask"])
    m3 = d["mask"].reshape(N).view(np.uint8)
    mask3_k = np.stack([m3[:P], np.concatenate([m3[P:], m3[P:]])], 1)
    mask3_row = np.stack([m3] * P)

    nc = bacc.Bacc("TRN2", target_bir_lowering=False, num_devices=1)
    arrays = {}

    def dram_in(name, array):
        arrays[name] = np.ascontiguousarray(array)
        return nc.dram_tensor(name, array.shape, mybir.dt.from_np(array.dtype), kind="ExternalInput").ap()

    x_ap = dram_in("x", to_tiles(get["x"][0]))
    params_ap = [{n: dram_in(f"l{l}_{n}", v) for n, v in layers[l].items()} for l in range(LAYERS)]
    consts_ap = dram_in("consts", shape_constants())
    mask3_k_ap, mask3_row_ap = dram_in("mask3_k", mask3_k), dram_in("mask3_row", mask3_row)
    out_ap = nc.dram_tensor("out", (TILES, P, TILE), F32, kind="ExternalOutput").ap()
    build_triangle_layers(nc, x_ap, params_ap, consts_ap, mask3_k_ap, mask3_row_ap, out_ap)
    r = run_bass_kernel_spmd(nc, [arrays], core_ids=[0])
    out = r.results[0]["out"].reshape(TILES, 2, C, ROWS, N)
    return np.ascontiguousarray(out.transpose(4, 1, 0, 3, 2)).reshape(1, N, N, C)
```

```python
from contextlib import ExitStack

import concourse.bass as bass
from concourse import mybir

F32 = mybir.dt.float32
BF16 = mybir.dt.bfloat16
U8 = mybir.dt.uint8
ALU = mybir.AluOpType
ACT = mybir.ActivationFunctionType

P = 128
C = 64
N = 192
HALF = N // 2
ROWS = 2
TILE = ROWS * N
TILES = HALF // ROWS
TAIL = N - P
COLS = 3 * C
RING = 4
TURNS = TILES // RING
SUBS = ROWS * TILES
GROUP = 4
GROUPS = C // GROUP
CHUNKS = TILE // P
LAYERS = 4
GN_EPS = 1e-5
LN_EPS = 1e-5

LN_W, LN_B, GATE_B, LN2_W, LN2_B, OUT_B, NCOL = 0, 1, 2, 3, 4, 5, 6
K_CENTRE, K_GROUP, K_IDENT, K_SEL, K_PARITY, K_PART, NCONST = 0, 128, 256, 384, 386, 514, 517

HAS_LN = (True, True, True, False)
HAS_BIAS = (True, True, True, False)
IN_PARTS = (False, True, True, True)
HAS_MASK = (True, True, False, True)
GATE_FIRST = (True, False, True, False)
T_SCALE = (1.0, 1.0, 1.0 / N, 1.0)


def build_triangle_layers(nc, x_in, params, consts, mask3_k, mask3_row, x_out):
    scratch = nc.dram_tensor("x_scratch", [TILES, P, TILE], F32).ap()
    gate_dram = nc.dram_tensor("gate_scratch", [TILES, P, TILE], F32).ap()
    t_f32 = nc.dram_tensor("t_scratch", [C, N * N], F32).ap()
    t_bf16 = nc.dram_tensor("t_scratch_bf16", [C, N * N], BF16).ap()

    with ExitStack() as ctx:
        def sb(name, shape, dt=F32):
            return ctx.enter_context(nc.sbuf_tensor(name, shape, dt))

        def sem(name):
            return ctx.enter_context(nc.semaphore(name))

        def sems(name, n=RING):
            return [sem(f"{name}{i}") for i in range(n)]

        lr = sb("lr", [P, COLS * N])
        in_ring = sb("in_ring", [P, RING, TILE])
        res_ring = sb("res_ring", [P, RING, TILE])
        gate_ring = sb("gate_ring", [P, RING, TILE])
        new_ring = sb("new_ring", [P, RING, TILE])
        cen = sb("cen", [P, RING, TILE])
        sq = sb("sq", [P, 2, TILE])
        rb = sb("rb", [P, 2, TILE])
        xn = sb("xn", [P, 2, TILE])
        act_out = sb("act_out", [P, 2, TILE])
        val = sb("val", [P, 2, TILE])
        w_parts = sb("w_parts", [P, 2, 2, 512], BF16)
        w_bias = sb("w_bias", [P, 2 * COLS])
        w_gate = sb("w_gate", [P, P])
        w_gate_parts = sb("w_gate_parts", [P, 2, P], BF16)
        w_out = sb("w_out", [P, P])
        w_out_s = sb("w_out_s", [P, 2, P])
        cols = sb("cols", [P, 2, NCOL])
        lnb6 = sb("lnb6", [P, 6])
        pb6 = sb("pb6", [6, 2 * COLS])
        bias_part = sb("bias_part", [6, 2, 2 * COLS], BF16)
        bias_rows = sb("bias_rows", [6, 2 * COLS], BF16)
        gate_bias = sb("gate_bias", [P, 1])
        out_bias = sb("out_bias", [P, 2])
        mask = sb("mask", [P, 2, N])
        mask_k8 = sb("mask_k8", [P, 2], U8)
        mask_k = sb("mask_k", [P, 2])
        mask_row8 = sb("mask_row8", [P, N], U8)
        k = sb("k", [P, NCONST])
        centre_bf = sb("centre_bf", [P, P], BF16)
        parity_bf = sb("parity_bf", [6, P], BF16)
        w_centre = sb("w_centre", [P, P])
        half_col = sb("half_col", [P, 2 * CHUNKS])
        ve = sb("ve", [P, 2, 2 * CHUNKS])
        rstd = sb("rstd", [P, 2, 2 * CHUNKS])
        stats = sb("stats", [P, TILES, 6])
        mv = sb("mv", [P, 2])
        gn = sb("gn", [P, 8])
        ps = ctx.enter_context(nc.psum_tensor("ps", [P, 8, 512], F32))

        xn_parts = val[:, :, :].bitcast(BF16).rearrange("p s (a f) -> p s a f", a=2)
        w_whole = w_parts[:, :, :, :].rearrange("p a h f -> p (a h f)").bitcast(F32).rearrange("p (h f) -> p h f", h=2)
        w_proj = new_ring[:, 0:2, :].rearrange("p a b -> p (a b)")[:, 0:512]
        bias_f = new_ring[0:6, 2:4, :]

        k_centre = k[:, K_CENTRE:K_CENTRE + P]
        k_group = k[:, K_GROUP:K_GROUP + P]
        k_ident = k[:, K_IDENT:K_IDENT + P]
        k_sel = k[:, K_SEL:K_SEL + 2]
        gn_mean, gn_dev, gn_q, gn_ve, gn_a, gn_b, gn_cb = (gn[:, i:i + 1] for i in range(7))

        in_loaded, res_loaded, gate_loaded = sems("in_loaded"), sems("res_loaded"), sems("gate_loaded")
        gate_stored, new_stored = sems("gate_stored"), sems("new_stored")
        planes_stored = sems("planes_stored", 2)
        consts_loaded, params_loaded, turned_stored = sem("consts_loaded"), sem("params_loaded"), sem("turned_stored")
        consts_ready, bias_mm, params_chain, params_ready = (
            sem("consts_ready"), sem("bias_mm"), sem("params_chain"), sem("params_ready"))
        mask_ready = sem("mask_ready")
        stats_done, gn_dve, gn_pe, gn_pool = sem("stats_done"), sem("gn_dve"), sem("gn_pe"), sem("gn_pool")
        a_z, a_cen, a_sq, a_var, a_ve, a_rstd, a_rb, a_bc, a_xn = (
            sem("a_" + s) for s in ("z", "cen", "sq", "var", "ve", "rstd", "rb", "bc", "xn"))
        a_hi, a_lo = sem("a_hi"), sem("a_lo")
        a_gate_mm, a_gate, a_proj, a_sig, a_masked, a_free = (
            sem("a_" + s) for s in ("gate_mm", "gate", "proj", "sig", "masked", "free"))
        b1_mm, b1_main, b1_tail = sem("b1_mm"), sem("b1_main"), sem("b1_tail")
        b2_z, b2_cen, b2_sq, b2_var, b2_ve, b2_rstd, b2_rb, b2_bc, b2_zn = (
            sem("b2_" + s) for s in ("z", "cen", "sq", "var", "ve", "rstd", "rb", "bc", "zn"))
        b2_aff, b2_val, b2_out, b2_gated, b2_new, b2_stat, b2_turned = (
            sem("b2_" + s) for s in ("aff", "val", "out", "gated", "new", "stat", "turned"))

        def x_src(l):
            return x_in if l == 0 else scratch

        def x_dst(l):
            return x_out if l == LAYERS - 1 else scratch

        def lr_view(l):
            flat = lr[:, :].bitcast(BF16)[:, 0:COLS * N] if l == 0 else lr[:, :]
            return flat.rearrange("p (c r) -> p c r", r=N)

        turned = lr[:, 0:N * HALF].rearrange("p (j i) -> p j i", i=HALF)

        def t_dram(l):
            return t_bf16 if l == 0 else t_f32

        def t_tile(l, n):
            return t_dram(l).rearrange("c (h t f) -> h c t f", h=2, f=TILE)[:, :, n, :]

        def t_slot(l, s):
            return in_ring[:, s, :].bitcast(BF16)[:, 0:TILE] if l == 0 else in_ring[:, s, :]

        def plane_out(l, g):
            main = in_ring[:, 2 * g:2 * g + 2, :].rearrange("p a b -> p (a b)")
            tail = cen[:, g, :]
            if l == 0:
                main, tail = main.bitcast(BF16)[:, 0:GROUP * N], tail.bitcast(BF16)[:, 0:2 * N]
            return main.rearrange("p (d q) -> p d q", q=N), tail.rearrange("p (d q) -> p d q", q=N)

        def in_count(l, phase):
            turns = TURNS
            return 16 * turns * (1 + 3 * l + phase)

        n_params = [7 + (1 if l < 2 else (2 if HAS_MASK[l] else 0)) for l in range(LAYERS)]

        def params_count(l):
            return 16 * sum(n_params[:l + 1])

        def gated_before(l):
            return sum(TILES for m in range(l) if not GATE_FIRST[m])

        def val_before(l):
            return sum(TILES for m in range(l) if GATE_FIRST[m])

        def parts_before(l):
            return sum(TILES for m in range(l) if IN_PARTS[m])

        def masked_before(l):
            return sum(SUBS for m in range(l) if HAS_MASK[m])

        def slot_free(eng, semaphore, value):
            if not (isinstance(value, int) and value <= 0):
                eng.wait_ge(semaphore, value)

        def over_tiles(eng, step, reach=RING):
            last = TURNS - reach // RING
            for s in range(RING):
                step(s, 0, s, TILES - 1 - s)
            with eng.Fori(1, last) as i:
                for s in range(RING):
                    step(i * RING + s, i, s, reach)
            for n in range(last * RING, TILES):
                step(n, n // RING, n % RING, TILES - 1 - n)

        block = ctx.enter_context(nc.Block())

        @block.sync
        def _(sp):
            sp.dma_start(k[:, :], consts).then_inc(consts_loaded, 16)

            def load_params(l):
                pr = params[l]
                sp.dma_start(w_proj, pr["w_proj"]).then_inc(params_loaded, 16)
                dst = [(w_bias, "w_bias"), (w_gate, "w_gate"), (w_out, "w_out"),
                       (lnb6, "lnb6"), (pb6, "pb6")]
                for tile, name in dst:
                    sp.dma_start(tile[:, :], pr[name]).then_inc(params_loaded, 16)
                sp.dma_start(cols[:, l % 2, :], pr["cols"]).then_inc(params_loaded, 16)
                if "mask" in pr:
                    sp.dma_start(mask[:, :, :], pr["mask"]).then_inc(params_loaded, 16)
                elif HAS_MASK[l]:
                    sp.dma_start(mask_k8[:, :], mask3_k).then_inc(params_loaded, 16)
                    sp.dma_start(mask_row8[:, :], mask3_row).then_inc(params_loaded, 16)

            def load_x(n, i, s):
                sp.wait_ge(stats_done, n - RING + 1)
                sp.dma_start(in_ring[:, s, :], x_in[n, :, :]).then_inc(in_loaded[s], 16)

            def phase_a(l):
                src, used = x_src(l), (a_z if HAS_LN[l] else a_xn)
                lead = RING - 1 if HAS_LN[l] else 1

                def load(n, s):
                    sp.dma_start(in_ring[:, s, :], src[n, :, :]).then_inc(in_loaded[s], 16)

                def step(n, i, s, ahead):
                    if ahead >= RING + lead:
                        sp.wait_ge(used, l * TILES + n + lead + 1)
                        load(n + lead + RING, (s + lead) % RING)
                    sp.wait_ge(a_gate, l * TILES + n + 1)
                    sp.dma_start(gate_dram[n, :, :], gate_ring[:, s, :]).then_inc(gate_stored[s], 16)

                for n in range(RING):
                    load(n, n)
                for n in range(lead):
                    sp.wait_ge(used, l * TILES + n + 1)
                    load(RING + n, n)
                over_tiles(sp, step, 2 * RING)

            def phase_b1(l):
                dram = t_dram(l).rearrange("(g d) (i j) -> g i d j", d=GROUP, j=N)
                for g in range(GROUPS):
                    main, tail = plane_out(l, g % 2)
                    sp.wait_ge(b1_main, l * GROUPS + g + 1)
                    sp.dma_start(dram[g, 0:P, :, :], main).then_inc(planes_stored[g % 2], 16)
                    sp.wait_ge(b1_tail, l * GROUPS + g + 1)
                    for e in range(2):
                        sp.dma_start(dram[g, P:N, e::2, :], tail[TAIL * e:TAIL * e + TAIL, :, :])\
                            .then_inc(planes_stored[g % 2], 16)

            def phase_b2(l):
                src, dst = x_src(l), x_dst(l)
                for s in range(2):
                    sp.wait_ge(planes_stored[s], (l + 1) * 48 * (GROUPS // 2))
                for s in range(RING):
                    sp.wait_ge(gate_stored[s], (l + 1) * 16 * TURNS)

                def load_t(n, s):
                    for h in range(2):
                        sp.dma_start(t_slot(l, s)[C * h:C * h + C, :], t_tile(l, n)[h, :, :]).then_inc(in_loaded[s], 16)

                def load_late(n, s):
                    sp.dma_start(res_ring[:, s, :], src[n, :, :]).then_inc(res_loaded[s], 16)
                    sp.dma_start(gate_ring[:, s, :], gate_dram[n, :, :]).then_inc(gate_loaded[s], 16)

                for n in range(RING):
                    load_t(n, n)
                    load_late(n, n)
                for n in range(RING):
                    sp.wait_ge(b2_z, l * TILES + n + 1)
                    load_t(RING + n, n)

                def step(n, i, s, ahead):
                    if ahead >= 2 * RING:
                        sp.wait_ge(b2_z, l * TILES + n + RING + 1)
                        load_t(n + 2 * RING, s)
                    sp.wait_ge(b2_new, l * TILES + n + 1)
                    if l != 1:
                        sp.dma_start(dst[n, :, :], new_ring[:, s, :]).then_inc(new_stored[s], 16)
                    if ahead >= RING:
                        load_late(n + RING, s)

                over_tiles(sp, step, 2 * RING)
                if l == 1:
                    sp.wait_ge(b2_turned, TILES)
                    for h in range(2):
                        for h2 in range(2):
                            for r in range(ROWS):
                                s_ap = turned[C * h:C * h + C, h2 * HALF + r:(h2 + 1) * HALF:ROWS, :]
                                d_ap = scratch.rearrange("t (h c) (r h2 i) -> h h2 r c t i", h=2, r=ROWS, h2=2)
                                sp.dma_start(d_ap[h2, h, r, :, :, :], s_ap).then_inc(turned_stored, 16)
                    sp.wait_ge(turned_stored, 16 * 8)
                else:
                    stores = sum(1 for m in range(l + 1) if m != 1)
                    for s in range(RING):
                        sp.wait_ge(new_stored[s], stores * 16 * TURNS)

            load_params(0)
            for s in range(RING):
                sp.dma_start(in_ring[:, s, :], x_in[s, :, :]).then_inc(in_loaded[s], 16)
            with sp.Fori(1, TURNS) as i:
                for s in range(RING):
                    load_x(i * RING + s, i, s)
            sp.wait_ge(stats_done, TILES)
            for l in range(LAYERS):
                phase_a(l)
                sp.wait_ge(a_free, (l + 1) * SUBS + 2)
                if l + 1 < LAYERS:
                    load_params(l + 1)
                phase_b1(l)
                phase_b2(l)

        @block.tensor
        def _(pe):
            def params_biases(l):
                pe.wait_ge(params_loaded, params_count(l))
                nc.tensor.matmul(ps[0:6, 7, 0:2 * COLS], lnb6[:, :], w_bias[:, :], start=True, stop=True)
                nc.tensor.matmul(ps[:, 7, 400:401], w_gate[:, :], cols[:, l % 2, LN_B:LN_B + 1], start=True, stop=True)
                nc.tensor.matmul(ps[:, 7, 402:403], w_out[:, :], cols[:, l % 2, LN2_B:LN2_B + 1],
                                 start=True, stop=True).then_inc(bias_mm, 1)

            def group_norm(l):
                pe.wait_ge(gn_dve, 7 * l + 1)
                nc.tensor.matmul(ps[:, 6, 0:1], k_group, mv[:, 0:1], start=True, stop=True).then_inc(gn_pe, 1)
                pe.wait_ge(gn_dve, 7 * l + 4)
                nc.tensor.matmul(ps[:, 6, 2:3], k_group, gn_q, start=True, stop=True).then_inc(gn_pe, 1)
                pe.wait_ge(gn_dve, 7 * l + 6)
                nc.tensor.matmul(ps[:, 6, 4:5], k_centre, gn_b, start=True, stop=True).then_inc(gn_pe, 1)

            def phase_a(l):
                base = l * TILES
                ln = HAS_LN[l]
                pe.wait_ge(gn_dve, 7 * (l + 1))
                pe.wait_ge(params_ready, l + 1)

                passes = ((0, 0), (1, 0), (0, 1)) if IN_PARTS[l] else ((0, 0),)

                def moving(part, s):
                    return xn_parts[:, s % 2, part, :] if IN_PARTS[l] else xn[:, s % 2, :]

                def gate_weights(part):
                    return w_gate_parts[:, part, :] if IN_PARTS[l] else w_gate[:, :]

                def proj_weights(part, h):
                    return w_parts[:, part, h, :] if IN_PARTS[l] else w_whole[:, h, :]

                def centre(n, i, s):
                    pe.wait_ge(in_loaded[s], in_count(l, 0) + 16 * (i + 1))
                    slot_free(pe, a_sq, base + n - 1)
                    nc.tensor.matmul(ps[:, s % 2, 0:TILE], w_centre[:, :], in_ring[:, s, :],
                                     start=True, stop=True).then_inc(a_z, 1)

                def variance(n, s):
                    pe.wait_ge(a_sq, base + n + 1)
                    slot_free(pe, a_xn, base + n - 1)
                    for j in range(CHUNKS):
                        mm = nc.tensor.matmul(ps[:, 2, TILE + 2 * j:TILE + 2 * j + 2],
                                              sq[:, s % 2, P * j:P * j + P], k_sel, start=True, stop=True)
                    mm.then_inc(a_var, 1)

                def spread(n, s, newest):
                    pe.wait_ge(a_rb, base + n + 1)
                    pe.wait_ge(a_ve, base + newest + 1)
                    for j in range(CHUNKS):
                        mm = nc.tensor.transpose(ps[:, 2, P * j:P * j + P], rb[:, s % 2, P * j:P * j + P], k_ident)
                    mm.then_inc(a_bc, 1)

                def gate(n, s):
                    if IN_PARTS[l]:
                        pe.wait_ge(a_lo, parts_before(l) + n + 1)
                    else:
                        pe.wait_ge(a_xn, base + n + 1)
                    slot_free(pe, a_gate, base + n)
                    for w, x in passes:
                        mm = nc.tensor.matmul(ps[:, 3, 0:TILE], gate_weights(w), moving(x, s),
                                              start=(w, x) == passes[0], stop=(w, x) == passes[-1])
                    mm.then_inc(a_gate_mm, 1)

                def project(n, s, r):
                    m = ROWS * n + r
                    pe.wait_ge(a_free, l * SUBS + m + 1)
                    banks = [ps[:, 4 + 2 * r + h, 0:2 * COLS].rearrange("p (v c) -> p v c", v=2) for h in range(2)]
                    if HAS_BIAS[l]:
                        for h in range(2):
                            nc.tensor.matmul(ps[:, 4 + 2 * r + h, 0:2 * COLS], parity_bf[:, :], bias_rows[:, :],
                                             start=True, stop=False, skip_group_check=True)
                    for w, x in passes:
                        start, stop = not HAS_BIAS[l] and (w, x) == passes[0], (w, x) == passes[-1]
                        for h in range(2):
                            nc.tensor.matmul(banks[h][:, :, 0:P], moving(x, s)[:, N * r:N * r + P],
                                             proj_weights(w, h)[:, 0:2 * P], start=start, stop=stop,
                                             skip_group_check=True)
                    for w, x in passes:
                        start, stop = not HAS_BIAS[l] and (w, x) == passes[0], (w, x) == passes[-1]
                        for h in range(2):
                            for e in range(2):
                                mm = nc.tensor.matmul(banks[h][TAIL * e:TAIL * e + TAIL, :, P:COLS],
                                                      moving(x, s)[:, N * r + P:N * r + N],
                                                      proj_weights(w, h)[:, 2 * P + P * e:3 * P + P * e],
                                                      start=start, stop=stop, skip_group_check=True)
                    mm.then_inc(a_proj, 1)

                def step(n, i, s, ahead):
                    if ln and ahead >= 2:
                        variance(n + 2, (s + 2) % RING)
                    if ln and ahead >= 1:
                        spread(n + 1, (s + 1) % RING, n + min(ahead, 2))
                    gate(n, s)
                    project(n, s, 0)
                    if ln and ahead >= 3:
                        centre(n + 3, i + (s + 3) // RING, (s + 3) % RING)
                    project(n, s, 1)

                if ln:
                    for n in range(3):
                        centre(n, 0, n)
                    variance(0, 0)
                    pe.wait_ge(a_ve, base + 1)
                    variance(1, 1)
                    spread(0, 0, 1)
                over_tiles(pe, step)

            def phase_b1(l):
                v = lr_view(l)
                pe.wait_ge(a_free, (l + 1) * SUBS + 2)

                def main_lr(d):
                    return v[:, d, :], v[:, C + d, :]

                def tail_lr(d):
                    e = d % 2
                    return (v[TAIL * e:TAIL * e + TAIL, 2 * C + d // 2, :],
                            v[TAIL * e:TAIL * e + TAIL, 2 * C + C // 2 + d // 2, :])

                for g in range(GROUPS):
                    b = 3 * (g % 2)
                    if g >= 2:
                        pe.wait_ge(b1_main, l * GROUPS + g - 1)
                        pe.wait_ge(b1_tail, l * GROUPS + g - 1)
                    for pair in range(2):
                        even, odd = GROUP * g + 2 * pair, GROUP * g + 2 * pair + 1
                        q = slice(N * pair, N * pair + N)
                        for part, (lo, hi) in ((main_lr, (True, False)), (tail_lr, (False, True))):
                            for e, d in enumerate((even, odd)):
                                left, right = part(d)
                                nc.tensor.matmul(ps[:, b + e, q], left[:, 0:P], right, start=lo, stop=hi)
                        for part, d, lo in ((tail_lr, even, True), (main_lr, odd, True),
                                            (main_lr, even, False), (tail_lr, odd, False)):
                            e = d % 2
                            left, right = part(d)
                            mm = nc.tensor.matmul(ps[TAIL * e:TAIL * e + TAIL, b + 2, q], left[:, P:N], right,
                                                  start=lo, stop=not lo, skip_group_check=True)
                    mm.then_inc(b1_mm, 1)

            def phase_b2(l):
                base = l * TILES
                w_c = centre_bf[:, :] if l == 0 else k_centre

                def centre(n, i, s):
                    pe.wait_ge(in_loaded[s], in_count(l, 1) + 32 * (i + 1))
                    slot_free(pe, b2_sq, base + n - 1)
                    nc.tensor.matmul(ps[:, s % 2, 0:TILE], w_c, t_slot(l, s), start=True, stop=True).then_inc(b2_z, 1)

                def variance(n, s):
                    pe.wait_ge(b2_sq, base + n + 1)
                    slot_free(pe, b2_ve, base + n - 1)
                    for j in range(CHUNKS):
                        mm = nc.tensor.matmul(ps[:, 6 + s % 2, 2 * j:2 * j + 2],
                                              sq[:, s % 2, P * j:P * j + P], k_sel, start=True, stop=True)
                    mm.then_inc(b2_var, 1)

                def spread(n, s):
                    pe.wait_ge(b2_rb, base + n + 1)
                    slot_free(pe, b2_zn, base + n - 1)
                    for j in range(CHUNKS):
                        mm = nc.tensor.transpose(ps[:, 2 + s % 2, P * j:P * j + P], rb[:, s % 2, P * j:P * j + P],
                                                 k_ident)
                    mm.then_inc(b2_bc, 1)

                def out(n, s):
                    if GATE_FIRST[l]:
                        pe.wait_ge(b2_val, val_before(l) + n + 1)
                    else:
                        pe.wait_ge(b2_zn, base + n + 1)
                    if GATE_FIRST[l]:
                        slot_free(pe, b2_new, base + n - 1)
                    else:
                        slot_free(pe, b2_gated, gated_before(l) + n - 1)
                    nc.tensor.matmul(ps[:, 4 + s % 2, 0:TILE], w_out_s[:, l % 2, :],
                                     (val if GATE_FIRST[l] else xn)[:, s % 2, :], start=True, stop=True)\
                        .then_inc(b2_out, 1)

                lead = 0 if GATE_FIRST[l] else 1

                def step(n, i, s, ahead):
                    if ahead >= 3:
                        variance(n + 3, (s + 3) % RING)
                    if ahead >= 4:
                        centre(n + 4, i + 1, s)
                    if ahead >= 2:
                        spread(n + 2, (s + 2) % RING)
                    if ahead >= lead:
                        out(n + lead, (s + lead) % RING)

                if l + 1 < LAYERS:
                    pe.wait_ge(params_ready, l + 2)
                for n in range(4):
                    centre(n, 0, n)
                for n in range(3):
                    variance(n, n)
                for n in range(2):
                    spread(n, n)
                if lead:
                    out(0, 0)
                over_tiles(pe, step)

            pe.wait_ge(consts_ready, 1)
            params_biases(0)
            group_norm(0)
            for l in range(LAYERS):
                phase_a(l)
                phase_b1(l)
                if l + 1 < LAYERS:
                    params_biases(l + 1)
                phase_b2(l)
                if l + 1 < LAYERS:
                    group_norm(l + 1)

        @block.scalar
        def _(act):
            def phase_a(l):
                base = l * TILES
                ln = HAS_LN[l]
                act.wait_ge(gn_dve, 7 * (l + 1))
                act.wait_ge(params_ready, l + 1)

                def centred(n, s):
                    act.wait_ge(a_z, base + n + 1)
                    slot_free(act, a_xn, base + n - RING + 1)
                    slot_free(act, a_var, base + n - 1)
                    nc.scalar.activation(cen[:, s, :], ps[:, s % 2, 0:TILE], ACT.Identity, bias=gn_cb)\
                        .then_inc(a_cen, 1)
                    nc.scalar.activation(sq[:, s % 2, :], ps[:, s % 2, 0:TILE], ACT.Square, bias=gn_cb)\
                        .then_inc(a_sq, 1)

                def spread(n, s):
                    act.wait_ge(a_rstd, base + n + 1)
                    slot_free(act, a_bc, base + n - 1)
                    nc.scalar.activation(rb[:, s % 2, :].rearrange("p (a c) -> p a c", c=C),
                                         rstd[:, s % 2, :].rearrange("p (a o) -> p a o", o=1)
                                         .broadcast_to([P, 2 * CHUNKS, C]), ACT.Copy).then_inc(a_rb, 1)

                def plain(n, i, s):
                    act.wait_ge(in_loaded[s], in_count(l, 0) + 16 * (i + 1))
                    slot_free(act, a_lo, parts_before(l) + n - 1)
                    nc.scalar.activation(xn[:, s % 2, :], in_ring[:, s, :], ACT.Identity, bias=gn_b, scale=gn_a)\
                        .then_inc(a_xn, 1)

                def gate(n, i, s):
                    act.wait_ge(a_gate_mm, base + n + 1)
                    slot_free(act, gate_stored[s], 16 * (l * TURNS + i))
                    nc.scalar.activation(gate_ring[:, s, :], ps[:, 3, 0:TILE], ACT.Sigmoid, bias=gate_bias[:, 0:1])\
                        .then_inc(a_gate, 1)

                def sigmoids(n, s, r):
                    m = ROWS * n + r
                    act.wait_ge(a_proj, l * SUBS + m + 1)
                    act.wait_ge(a_free, l * SUBS + m + 1)
                    nc.scalar.activation(act_out[:, r, :].rearrange("p (h c) -> p h c", h=2),
                                         ps[:, 4 + 2 * r:6 + 2 * r, COLS:2 * COLS], ACT.Sigmoid).then_inc(a_sig, 1)

                def high(n, s):
                    act.wait_ge(a_xn, base + n + 1)
                    slot_free(act, a_proj, l * SUBS + ROWS * (n - 1))
                    nc.scalar.activation(xn_parts[:, s % 2, 0, :], xn[:, s % 2, :], ACT.Copy).then_inc(a_hi, 1)

                def step(n, i, s, ahead):
                    gate(n, i, s)
                    if not ln and ahead >= 1:
                        plain(n + 1, i + (s + 1) // RING, (s + 1) % RING)
                    if IN_PARTS[l] and ahead >= 1:
                        high(n + 1, (s + 1) % RING)
                    sigmoids(n, s, 0)
                    if ln and ahead >= 3:
                        centred(n + 3, (s + 3) % RING)
                    if ln and ahead >= 2:
                        spread(n + 2, (s + 2) % RING)
                    sigmoids(n, s, 1)

                if ln:
                    centred(0, 0)
                    centred(1, 1)
                    spread(0, 0)
                    centred(2, 2)
                    if IN_PARTS[l]:
                        high(0, 0)
                    spread(1, 1)
                else:
                    plain(0, 0, 0)
                    high(0, 0)
                over_tiles(act, step)

            def phase_b1(l):
                for g in range(GROUPS):
                    main, _ = plane_out(l, g % 2)
                    act.wait_ge(b1_mm, l * GROUPS + g + 1)
                    if g >= 2:
                        act.wait_ge(planes_stored[g % 2], 48 * (l * (GROUPS // 2) + g // 2))
                    b = 3 * (g % 2)
                    nc.scalar.activation(main.rearrange("p (a e) q -> p e a q", e=2),
                                         ps[:, b:b + 2, 0:2 * N].rearrange("p e (a q) -> p e a q", q=N),
                                         ACT.Copy).then_inc(b1_main, 1)

            def phase_b2(l):
                base = l * TILES

                def centred(n, s):
                    act.wait_ge(b2_z, base + n + 1)
                    slot_free(act, b2_zn, base + n - RING + 1)
                    slot_free(act, b2_var, base + n - 1)
                    nc.scalar.activation(cen[:, s, :], ps[:, s % 2, 0:TILE], ACT.Copy, scale=T_SCALE[l])\
                        .then_inc(b2_cen, 1)
                    nc.scalar.activation(sq[:, s % 2, :], ps[:, s % 2, 0:TILE], ACT.Square, scale=T_SCALE[l])\
                        .then_inc(b2_sq, 1)

                def spread(n, s):
                    act.wait_ge(b2_rstd, base + n + 1)
                    slot_free(act, b2_bc, base + n - 1)
                    nc.scalar.activation(rb[:, s % 2, :].rearrange("p (a c) -> p a c", c=C),
                                         rstd[:, s % 2, :].rearrange("p (a o) -> p a o", o=1)
                                         .broadcast_to([P, 2 * CHUNKS, C]), ACT.Copy).then_inc(b2_rb, 1)

                def affine(n, s):
                    act.wait_ge(b2_zn, base + n + 1)
                    slot_free(act, b2_val, val_before(l) + n - 1)
                    nc.scalar.activation(act_out[:, s % 2, :], xn[:, s % 2, :], ACT.Identity,
                                         bias=cols[:, l % 2, LN2_B:LN2_B + 1],
                                         scale=cols[:, l % 2, LN2_W:LN2_W + 1]).then_inc(b2_aff, 1)

                def turn(n, s):
                    act.wait_ge(b2_new, base + n + 1)
                    nc.scalar.activation(turned[:, :, bass.ds(ROWS * n, ROWS)].rearrange("p j i -> p i j"),
                                         new_ring[:, s, :].rearrange("p (r j) -> p r j", r=ROWS),
                                         ACT.Copy).then_inc(b2_turned, 1)

                def step(n, i, s, ahead):
                    if ahead >= 2:
                        spread(n + 2, (s + 2) % RING)
                    if GATE_FIRST[l] and ahead >= 1:
                        affine(n + 1, (s + 1) % RING)
                    if l == 1 and not (isinstance(n, int) and n == 0):
                        turn(n - 1, (s - 1) % RING)
                    if ahead >= 4:
                        centred(n + 4, s)

                for n in range(4):
                    centred(n, n)
                for n in range(2):
                    spread(n, n)
                if GATE_FIRST[l]:
                    affine(0, 0)
                over_tiles(act, step)
                if l == 1:
                    turn(TILES - 1, RING - 1)

            for l in range(LAYERS):
                phase_a(l)
                phase_b1(l)
                phase_b2(l)

        @block.vector
        def _(dve):
            dve.sem_inc(a_free, 2)
            dve.wait_ge(consts_loaded, 16)
            nc.vector.memset(w_parts[:, :, :, :], 0.0)
            nc.vector.tensor_copy(centre_bf[:, :], k_centre)
            nc.vector.tensor_copy(parity_bf[:, :], k[0:6, K_PARITY:K_PARITY + P]).then_inc(consts_ready, 1)

            def params_scaled(l):
                c = cols[:, l % 2, :]
                chain = [10 * l - 2 * sum(not IN_PARTS[m] for m in range(l))]

                def link(ins):
                    chain[0] += 1
                    ins.then_inc(params_chain, 1)
                    dve.wait_ge(params_chain, chain[0])

                dve.wait_ge(params_loaded, params_count(l))
                dve.wait_ge(bias_mm, l + 1)
                link(nc.vector.tensor_tensor(bias_f[:, 0, :], ps[0:6, 7, 0:2 * COLS], pb6[:, :], ALU.add))
                link(nc.vector.tensor_copy(bias_part[:, 0, :], bias_f[:, 0, :]))
                link(nc.vector.tensor_tensor(bias_f[:, 1, :], bias_f[:, 0, :], bias_part[:, 0, :], ALU.subtract))
                link(nc.vector.tensor_copy(bias_part[:, 1, :], bias_f[:, 1, :]))
                link(nc.vector.tensor_tensor(bias_f[:, 0, :], bias_f[:, 1, :], bias_part[:, 1, :], ALU.subtract))
                link(nc.vector.tensor_scalar(bias_rows[:, :], bias_f[:, 0, :], k[0:6, K_PART + 2:K_PART + 3], None, ALU.mult))
                link(nc.vector.scalar_tensor_tensor(bias_rows[:, :], bias_part[:, 0, :], k[0:6, K_PART:K_PART + 1],
                                                    bias_rows[:, :], ALU.mult, ALU.add))
                nc.vector.scalar_tensor_tensor(bias_rows[:, :], bias_part[:, 1, :], k[0:6, K_PART + 1:K_PART + 2],
                                               bias_rows[:, :], ALU.mult, ALU.add)
                nc.vector.tensor_tensor(gate_bias[:, :], ps[:, 7, 400:401], c[:, GATE_B:GATE_B + 1], ALU.add)
                nc.vector.tensor_scalar(w_proj, w_proj, c[:, LN_W:LN_W + 1], None, ALU.mult)
                link(nc.vector.tensor_scalar(w_gate[:, :], w_gate[:, :], c[:, LN_W:LN_W + 1], None, ALU.mult))
                for h in range(2):
                    half = slice(C * h, C * h + C)
                    hi = w_parts[half, 0, h, :] if IN_PARTS[l] else w_whole[half, h, :]
                    nc.vector.tensor_copy(hi, w_proj[half, :])
                if IN_PARTS[l]:
                    if not IN_PARTS[l - 1]:
                        for h in range(2):
                            nc.vector.memset(w_parts[C - C * h:2 * C - C * h, :, h, :], 0.0)
                    link(nc.vector.tensor_copy(w_gate_parts[:, 0, :], w_gate[:, :]))
                    for h in range(2):
                        half = slice(C * h, C * h + C)
                        nc.vector.tensor_tensor(w_parts[half, 1, h, :], w_proj[half, :], w_parts[half, 0, h, :],
                                                ALU.subtract)
                    link(nc.vector.tensor_tensor(w_gate_parts[:, 1, :], w_gate[:, :], w_gate_parts[:, 0, :],
                                                 ALU.subtract))
                if HAS_MASK[l] and l >= 2:
                    nc.vector.tensor_copy(mask_k[:, :], mask_k8[:, :]).then_inc(mask_ready, 1)
                    dve.wait_ge(mask_ready, 1)
                    for t in range(2):
                        nc.vector.tensor_scalar(mask[:, t, :], mask_row8[:, :], mask_k[:, t:t + 1], None, ALU.mult)
                if GATE_FIRST[l]:
                    nc.vector.tensor_copy(out_bias[:, l % 2:l % 2 + 1], c[:, OUT_B:OUT_B + 1])
                    nc.vector.tensor_copy(w_out_s[:, l % 2, :], w_out[:, :]).then_inc(params_ready, 1)
                else:
                    nc.vector.tensor_tensor(out_bias[:, l % 2:l % 2 + 1], ps[:, 7, 402:403], c[:, OUT_B:OUT_B + 1], ALU.add)
                    nc.vector.tensor_scalar(w_out_s[:, l % 2, :], w_out[:, :], c[:, LN2_W:LN2_W + 1], None,
                                            ALU.mult).then_inc(params_ready, 1)

            def group_norm(l):
                b = 7 * l
                dve.wait_ge(stats_done, (l + 1) * TILES)
                nc.vector.bn_aggr(mv[:, :], stats[:, :, :].rearrange("p t s -> p (t s)")).then_inc(gn_dve, 1)
                dve.wait_ge(gn_pe, 3 * l + 1)
                nc.vector.tensor_copy(gn_mean, ps[:, 6, 0:1]).then_inc(gn_dve, 1)
                dve.wait_ge(gn_dve, b + 2)
                nc.vector.tensor_tensor(gn_dev, mv[:, 0:1], gn_mean, ALU.subtract).then_inc(gn_dve, 1)
                dve.wait_ge(gn_dve, b + 3)
                nc.vector.scalar_tensor_tensor(gn_q, gn_dev, gn_dev, mv[:, 1:2], ALU.mult, ALU.add).then_inc(gn_dve, 1)
                dve.wait_ge(gn_pe, 3 * l + 2)
                nc.vector.tensor_scalar(gn_ve, ps[:, 6, 2:3], GN_EPS, None, ALU.add).then_inc(gn_dve, 1)
                dve.wait_ge(gn_pool, l + 1)
                nc.vector.tensor_scalar(gn_b, gn_mean, gn_a, -1.0, ALU.mult, ALU.mult).then_inc(gn_dve, 1)
                nc.vector.tensor_scalar(w_centre[:, :], k_centre, gn_a, None, ALU.mult)
                dve.wait_ge(gn_pe, 3 * l + 3)
                nc.vector.tensor_copy(gn_cb, ps[:, 6, 4:5]).then_inc(gn_dve, 1)

            def phase_a(l):
                base = l * TILES
                ln = HAS_LN[l]
                out4 = lr_view(l).rearrange("p c (h r) -> p h c r", h=2)
                if l:
                    dve.wait_ge(b1_mm, l * GROUPS)
                if l == 2:
                    dve.wait_ge(turned_stored, 16 * 8)

                def var_eps(n, s):
                    dve.wait_ge(a_var, base + n + 1)
                    slot_free(dve, a_rstd, base + n - 1)
                    nc.vector.tensor_scalar(ve[:, s % 2, :], ps[:, 2, TILE:TILE + 2 * CHUNKS], LN_EPS, None,
                                            ALU.add).then_inc(a_ve, 1)

                def normalise(n, s):
                    dve.wait_ge(a_bc, base + n + 1)
                    dve.wait_ge(a_cen, base + n + 1)
                    if IN_PARTS[l]:
                        slot_free(dve, a_lo, parts_before(l) + n - 1)
                    else:
                        slot_free(dve, a_proj, l * SUBS + ROWS * (n - 1))
                    nc.vector.tensor_tensor(xn[:, s % 2, :], ps[:, 2, 0:TILE], cen[:, s, :], ALU.mult)\
                        .then_inc(a_xn, 1)

                def low(n, s):
                    dve.wait_ge(a_hi, parts_before(l) + n + 1)
                    nc.vector.tensor_tensor(xn_parts[:, s % 2, 1, :], xn[:, s % 2, :], xn_parts[:, s % 2, 0, :],
                                            ALU.subtract).then_inc(a_lo, 1)

                def glu(n, r):
                    m = ROWS * n + r
                    if HAS_MASK[l]:
                        dve.wait_ge(a_masked, masked_before(l) + m + 1)
                    else:
                        dve.wait_ge(a_sig, l * SUBS + m + 1)
                    nc.vector.tensor_tensor(out4[:, :, :, m], ps[:, 4 + 2 * r:6 + 2 * r, 0:COLS],
                                            act_out[:, r, :].rearrange("p (h c) -> p h c", h=2),
                                            ALU.mult).then_inc(a_free, 1)

                def step(n, i, s, ahead):
                    if ln and ahead >= 2:
                        var_eps(n + 2, (s + 2) % RING)
                    if ln and ahead >= 1:
                        normalise(n + 1, (s + 1) % RING)
                    if IN_PARTS[l] and ahead >= 1:
                        low(n + 1, (s + 1) % RING)
                    if not (isinstance(n, int) and n == 0):
                        glu(n - 1, 1)
                    glu(n, 0)

                if ln:
                    var_eps(0, 0)
                    var_eps(1, 1)
                    normalise(0, 0)
                if IN_PARTS[l]:
                    low(0, 0)
                over_tiles(dve, step)
                glu(TILES - 1, 1)

            def phase_b1(l):
                for g in range(GROUPS):
                    _, tail = plane_out(l, g % 2)
                    dve.wait_ge(b1_mm, l * GROUPS + g + 1)
                    if g >= 2:
                        dve.wait_ge(planes_stored[g % 2], 48 * (l * (GROUPS // 2) + g // 2))
                    nc.vector.tensor_copy(tail, ps[:, 3 * (g % 2) + 2, 0:2 * N].rearrange("p (a q) -> p a q", q=N))\
                        .then_inc(b1_tail, 1)

            def phase_b2(l):
                base = l * TILES

                def var_eps(n, s):
                    dve.wait_ge(b2_var, base + n + 1)
                    slot_free(dve, b2_rstd, base + n - 1)
                    nc.vector.tensor_scalar(ve[:, s % 2, :], ps[:, 6 + s % 2, 0:2 * CHUNKS], LN_EPS, None,
                                            ALU.add).then_inc(b2_ve, 1)

                def normalise(n, s):
                    dve.wait_ge(b2_bc, base + n + 1)
                    dve.wait_ge(b2_cen, base + n + 1)
                    if GATE_FIRST[l]:
                        slot_free(dve, b2_aff, val_before(l) + n - 1)
                    else:
                        slot_free(dve, b2_out, base + n - 1)
                    nc.vector.tensor_tensor(xn[:, s % 2, :], ps[:, 2 + s % 2, 0:TILE], cen[:, s, :], ALU.mult)\
                        .then_inc(b2_zn, 1)

                def finish(n, i, s):
                    bias = out_bias[:, l % 2:l % 2 + 1]
                    dve.wait_ge(b2_out, base + n + 1)
                    if GATE_FIRST[l]:
                        dve.wait_ge(res_loaded[s], 16 * (l * TURNS + i + 1))
                        slot_free(dve, new_stored[s], 16 * (l // 2 * TURNS + i))
                        nc.vector.scalar_tensor_tensor(new_ring[:, s, :], ps[:, 4 + s % 2, 0:TILE], bias,
                                                       res_ring[:, s, :], ALU.add, ALU.add).then_inc(b2_new, 1)
                    else:
                        dve.wait_ge(gate_loaded[s], 16 * (l * TURNS + i + 1))
                        slot_free(dve, b2_new, base + n - 1)
                        nc.vector.scalar_tensor_tensor(val[:, s % 2, :], ps[:, 4 + s % 2, 0:TILE], bias,
                                                       gate_ring[:, s, :], ALU.add, ALU.mult).then_inc(b2_gated, 1)

                def statistics(n, s):
                    dve.wait_ge(b2_new, base + n + 1)
                    nc.vector.bn_stats(stats[:, n, :], new_ring[:, s, :]).then_inc(stats_done, 1)

                lead = 0 if GATE_FIRST[l] else 1

                def step(n, i, s, ahead):
                    if ahead >= 3:
                        var_eps(n + 3, (s + 3) % RING)
                    if ahead >= 2:
                        normalise(n + 2, (s + 2) % RING)
                    if not (isinstance(n, int) and n == 0) and l + 1 < LAYERS:
                        statistics(n - 1, (s - 1) % RING)
                    if ahead >= lead:
                        finish(n + lead, i + (s + lead) // RING, (s + lead) % RING)

                for n in range(3):
                    var_eps(n, n)
                for n in range(2):
                    normalise(n, n)
                if lead:
                    finish(0, 0, 0)
                over_tiles(dve, step)
                if l + 1 < LAYERS:
                    statistics(TILES - 1, RING - 1)

            def first_statistics(i, s):
                dve.wait_ge(in_loaded[s], 16 * (i + 1))
                nc.vector.bn_stats(stats[:, i * RING + s, :], in_ring[:, s, :]).then_inc(stats_done, 1)

            params_scaled(0)
            with dve.Fori(0, TURNS) as i:
                for s in range(RING):
                    first_statistics(i, s)
            group_norm(0)
            for l in range(LAYERS):
                phase_a(l)
                phase_b1(l)
                if l + 1 < LAYERS:
                    params_scaled(l + 1)
                phase_b2(l)
                if l + 1 < LAYERS:
                    group_norm(l + 1)

        @block.gpsimd
        def _(pool):
            half_set = sem("half_set")
            nc.gpsimd.memset(half_col[:, :], -0.5).then_inc(half_set, 1)
            pool.wait_ge(half_set, 1)

            def group_norm(l):
                pool.wait_ge(gn_dve, 7 * l + 5)
                nc.gpsimd.tensor_tensor(gn_a, gn_ve, half_col[:, 0:1], ALU.pow).then_inc(gn_pool, 1)

            def phase_a(l):
                base = l * TILES
                ln = HAS_LN[l]
                mask4 = mask[:, :, :].rearrange("p t (h r) -> p t h r", h=2)
                pool.wait_ge(params_ready, l + 1)

                def inverse(n, s):
                    pool.wait_ge(a_ve, base + n + 1)
                    slot_free(pool, a_rb, base + n - 1)
                    nc.gpsimd.tensor_tensor(rstd[:, s % 2, :], ve[:, s % 2, :], half_col[:, :], ALU.pow)\
                        .then_inc(a_rstd, 1)

                def masked(n, r):
                    m = ROWS * n + r
                    pool.wait_ge(a_sig, l * SUBS + m + 1)
                    sig = act_out[:, r, :].rearrange("p (h c) -> p h c", h=2)
                    for t, (lo, hi) in enumerate(((0, P), (P, COLS))):
                        row = mask4[:, t, :, m].rearrange("p (h o) -> p h o", o=1).broadcast_to([P, 2, hi - lo])
                        ins = nc.gpsimd.tensor_tensor(sig[:, :, lo:hi], sig[:, :, lo:hi], row, ALU.mult)
                    ins.then_inc(a_masked, 1)

                def step(n, i, s, ahead):
                    if HAS_MASK[l] and not (isinstance(n, int) and n == 0):
                        masked(n - 1, 1)
                    if ln and ahead >= 2:
                        inverse(n + 2, (s + 2) % RING)
                    if HAS_MASK[l]:
                        masked(n, 0)

                if ln:
                    inverse(0, 0)
                    inverse(1, 1)
                over_tiles(pool, step)
                if HAS_MASK[l]:
                    masked(TILES - 1, 1)

            def phase_b2(l):
                base = l * TILES

                def inverse(n, s):
                    pool.wait_ge(b2_ve, base + n + 1)
                    slot_free(pool, b2_rb, base + n - 1)
                    nc.gpsimd.tensor_tensor(rstd[:, s % 2, :], ve[:, s % 2, :], half_col[:, :], ALU.pow)\
                        .then_inc(b2_rstd, 1)

                def gated(n, i, s):
                    pool.wait_ge(b2_aff, val_before(l) + n + 1)
                    pool.wait_ge(gate_loaded[s], 16 * (l * TURNS + i + 1))
                    slot_free(pool, b2_out, base + n - 1)
                    nc.gpsimd.tensor_tensor(val[:, s % 2, :], act_out[:, s % 2, :], gate_ring[:, s, :], ALU.mult)\
                        .then_inc(b2_val, 1)

                def residual(n, i, s):
                    pool.wait_ge(b2_gated, gated_before(l) + n + 1)
                    pool.wait_ge(res_loaded[s], 16 * (l * TURNS + i + 1))
                    if l == 1:
                        slot_free(pool, b2_turned, n - RING + 1)
                        slot_free(pool, stats_done, (l + 1) * TILES + n - RING + 1)
                    else:
                        pool.wait_ge(new_stored[s], 16 * (2 * TURNS + i))
                    nc.gpsimd.tensor_tensor(new_ring[:, s, :], val[:, s % 2, :], res_ring[:, s, :], ALU.add)\
                        .then_inc(b2_new, 1)

                def step(n, i, s, ahead):
                    if ahead >= 3:
                        inverse(n + 3, (s + 3) % RING)
                    if not GATE_FIRST[l]:
                        residual(n, i, s)
                    elif ahead >= 1:
                        gated(n + 1, i + (s + 1) // RING, (s + 1) % RING)

                for n in range(3):
                    inverse(n, n)
                if GATE_FIRST[l]:
                    gated(0, 0, 0)
                over_tiles(pool, step)

            group_norm(0)
            for l in range(LAYERS):
                phase_a(l)
                phase_b2(l)
                if l + 1 < LAYERS:
                    group_norm(l + 1)


def shape_constants():
    import numpy as np
    k = np.zeros((P, NCONST), np.float32)
    part = np.arange(P)
    same_half = part[:, None] // C == part[None, :] // C
    k[:, K_CENTRE:K_CENTRE + P] = np.eye(P) - same_half / C
    k[:, K_GROUP:K_GROUP + P] = (part[:, None] % C // 2 == part[None, :] % C // 2) / 4
    k[:, K_IDENT:K_IDENT + P] = np.eye(P)
    for h in range(2):
        k[C * h:C * h + C, K_SEL + h] = 1 / C
        k[3 * h:3 * h + 3, K_PARITY + TAIL * h:K_PARITY + TAIL * h + TAIL] = 1
    for r in range(6):
        k[r, K_PART + r % 3] = 1
    return k


def kernel(**inputs):
    import numpy as np
    import concourse.bacc as bacc
    from concourse.bass_utils import run_bass_kernel_spmd

    get = {name: np.asarray(a) for name, a in inputs.items()}

    def to_tiles(x):
        return np.ascontiguousarray(x.reshape(2, TILES, ROWS, N, C).transpose(1, 0, 4, 2, 3)).reshape(TILES, P, TILE)

    def blocks(w):
        out = np.zeros((P, P), np.float32)
        out[:C, :C] = w
        out[C:, C:] = w
        return out

    def params(l, left, right, left_g, right_g, gate, out, bias, ln, ln2, gate_b, out_b):
        values, gates = np.concatenate([left, right], 1), np.concatenate([left_g, right_g], 1)
        tails = [[np.concatenate([a[..., e::2], b[..., e::2]], -1) for a, b in ((left, right), (left_g, right_g))]
                 for e in range(2)]
        proj = np.concatenate([values, gates] + tails[0] + tails[1], 1)
        row = [np.concatenate([values, tails[e][0], gates, tails[e][1]], 1) for e in range(2)]
        bl, br, blg, brg = bias
        b_main = [np.concatenate([bl, br]), np.concatenate([blg, brg])]
        b_rows = [np.concatenate([b_main[0], bl[e::2], br[e::2], b_main[1], blg[e::2], brg[e::2]]) for e in range(2)]
        ln_w, ln_b = ln
        lnb6 = np.zeros((P, 6), np.float32)
        lnb6[:C, 0:3] = ln_b[:, None]
        lnb6[C:, 3:6] = ln_b[:, None]
        columns = np.stack([ln_w, ln_b, gate_b, ln2[0], ln2[1], out_b], 1)
        return {"w_proj": np.concatenate([proj, proj], 0), "w_bias": np.concatenate(row, 0),
                "w_gate": blocks(gate), "w_out": blocks(out), "lnb6": lnb6,
                "pb6": np.stack([b_rows[0]] * 3 + [b_rows[1]] * 3),
                "cols": np.concatenate([columns, columns], 0)}

    def mask_tiles(m):
        mt = m.reshape(N, N).T
        return np.stack([mt[:P], np.concatenate([mt[P:], mt[P:]], 0)], 1)

    zero, one = np.zeros(C, np.float32), np.ones(C, np.float32)
    a, b, c, d = ({n[8:]: v for n, v in get.items() if n.startswith(f"L{l}_conv_")} for l in range(LAYERS))
    layers = [
        params(0, a["Wl"].T, a["Wr"].T, a["Wlg"].T, a["Wrg"].T, a["Wog"].T, a["Wout"].T, (zero,) * 4,
               (a["ln1_w"], a["ln1_b"]), (a["ln2_w"], a["ln2_b"]), zero, zero),
        params(1, b["w_a_p"], b["w_b_p"], b["w_a_g"], b["w_b_g"], b["w_g"], b["w_o"],
               (b["b_a_p"], b["b_b_p"], b["b_a_g"], b["b_b_g"]),
               (b["ln_in_w"], b["ln_in_b"]), (b["ln_out_w"], b["ln_out_b"]), b["b_g"], b["b_o"]),
        params(2, c["Wl"], c["Wr"], c["Wlg"], c["Wrg"], c["Wog"], c["Wo"],
               (c["bl"], c["br"], c["blg"], c["brg"]),
               (c["norm_a"], c["norm_b"]), (c["on_a"], c["on_b"]), c["bog"], c["bo"]),
        params(3, d["W_lr"][:, 0:C], d["W_lr"][:, C:2 * C], d["W_lr"][:, 2 * C:3 * C], d["W_lr"][:, 3 * C:4 * C],
               d["W_gate"], d["W_out"], (zero,) * 4, (one, zero), (d["ln_w"], d["ln_b"]), zero, zero),
    ]
    layers[0]["mask"] = mask_tiles(a["mask"])
    layers[1]["mask"] = mask_tiles(b["mask"])
    m3 = d["mask"].reshape(N).view(np.uint8)
    mask3_k = np.stack([m3[:P], np.concatenate([m3[P:], m3[P:]])], 1)
    mask3_row = np.stack([m3] * P)

    nc = bacc.Bacc("TRN2", target_bir_lowering=False, num_devices=1)
    arrays = {}

    def dram_in(name, array):
        arrays[name] = np.ascontiguousarray(array)
        return nc.dram_tensor(name, array.shape, mybir.dt.from_np(array.dtype), kind="ExternalInput").ap()

    x_ap = dram_in("x", to_tiles(get["x"][0]))
    params_ap = [{n: dram_in(f"l{l}_{n}", v) for n, v in layers[l].items()} for l in range(LAYERS)]
    consts_ap = dram_in("consts", shape_constants())
    mask3_k_ap, mask3_row_ap = dram_in("mask3_k", mask3_k), dram_in("mask3_row", mask3_row)
    out_ap = nc.dram_tensor("out", (TILES, P, TILE), F32, kind="ExternalOutput").ap()
    build_triangle_layers(nc, x_ap, params_ap, consts_ap, mask3_k_ap, mask3_row_ap, out_ap)
    r = run_bass_kernel_spmd(nc, [arrays], core_ids=[0])
    out = r.results[0]["out"].reshape(TILES, 2, C, ROWS, N)
    return np.ascontiguousarray(out.transpose(4, 1, 0, 3, 2)).reshape(1, N, N, C)
```

```python
from contextlib import ExitStack

import concourse.bass as bass
from concourse import mybir

F32 = mybir.dt.float32
BF16 = mybir.dt.bfloat16
U8 = mybir.dt.uint8
ALU = mybir.AluOpType
ACT = mybir.ActivationFunctionType

P = 128
C = 64
N = 192
HALF = N // 2
ROWS = 2
TILE = ROWS * N
TILES = HALF // ROWS
TAIL = N - P
COLS = 3 * C
RING = 4
TURNS = TILES // RING
PAIRS = RING // 2
PIECES = 6
EARLY = 8
SUBS = ROWS * TILES
GROUP = 4
GROUPS = C // GROUP
CHUNKS = TILE // P
LAYERS = 4
GN_EPS = 1e-5
LN_EPS = 1e-5

LN_W, LN_B, GATE_B, LN2_W, LN2_B, OUT_B, NCOL = 0, 1, 2, 3, 4, 5, 6
K_CENTRE, K_GROUP, K_IDENT, K_SEL, NCONST = 0, 128, 256, 384, 386

HAS_LN = (True, True, True, False)
IN_PARTS = (False, True, True, True)
HAS_MASK = (True, True, False, True)
GATE_FIRST = (True, False, True, False)
T_SCALE = (1.0, 1.0, 1.0 / N, 1.0)


def build_triangle_layers(nc, x_in, params, consts, mask3_k, mask3_row, x_out):
    scratch = nc.dram_tensor("x_scratch", [TILES, P, TILE], F32).ap()
    gate_dram = nc.dram_tensor("gate_scratch", [TILES, P, TILE], F32).ap()
    t_f32 = nc.dram_tensor("t_scratch", [C, N * N], F32).ap()
    t_bf16 = nc.dram_tensor("t_scratch_bf16", [C, N * N], BF16).ap()

    with ExitStack() as ctx:
        def sb(name, shape, dt=F32):
            return ctx.enter_context(nc.sbuf_tensor(name, shape, dt))

        def sem(name):
            return ctx.enter_context(nc.semaphore(name))

        def sems(name, n=RING):
            return [sem(f"{name}{i}") for i in range(n)]

        lr = sb("lr", [P, COLS * N])
        in_ring = sb("in_ring", [P, RING, TILE])
        res_ring = sb("res_ring", [P, RING, TILE])
        gate_ring = sb("gate_ring", [P, RING, TILE])
        new_ring = sb("new_ring", [P, RING, TILE])
        cen = sb("cen", [P, RING, TILE])
        sq = sb("sq", [P, 2, TILE])
        sq_parts = sb("sq_parts", [P, 2, 2, TILE], BF16)
        rb = sb("rb", [P, 2, TILE])
        xn = sb("xn", [P, 2, TILE])
        act_out = sb("act_out", [P, 2, TILE])
        val = sb("val", [P, 2, TILE])
        w_parts = sb("w_parts", [P, 2, 2, 512], BF16)
        w_gate = sb("w_gate", [P, P])
        w_gate_parts = sb("w_gate_parts", [P, 2, P], BF16)
        w_out = sb("w_out", [P, P])
        w_out_s = sb("w_out_s", [P, 2, P])
        cols = sb("cols", [P, 2, NCOL])
        shift_col = sb("shift_col", [P, 1])
        averager = sb("averager", [P, P])
        shift_w = sb("shift_w", [P, P])
        gate_bias = sb("gate_bias", [P, 1])
        out_bias = sb("out_bias", [P, 2])
        mask = sb("mask", [P, 2, N])
        mask_k8 = sb("mask_k8", [P, 2], U8)
        mask_k = sb("mask_k", [P, 2])
        mask_row8 = sb("mask_row8", [P, N], U8)
        k = sb("k", [P, NCONST])
        centre_bf = sb("centre_bf", [P, P], BF16)
        sel_bf = sb("sel_bf", [P, 2], BF16)
        w_centre = sb("w_centre", [P, P])
        half_col = sb("half_col", [P, 2 * CHUNKS])
        eps_col = sb("eps_col", [P, 1])
        root_table = sb("root_table", [P, 1])
        ve = sb("ve", [P, 2, 2 * CHUNKS])
        rstd = sb("rstd", [P, 2, 2 * CHUNKS])
        stats = sb("stats", [P, TILES, 6])
        mv = sb("mv", [P, 2])
        gn = sb("gn", [P, 8])
        ps = ctx.enter_context(nc.psum_tensor("ps", [P, 8, 512], F32))

        xn_parts = val[:, :, :].bitcast(BF16).rearrange("p s (a f) -> p s a f", a=2)
        w_whole = w_parts[:, :, :, :].rearrange("p a h f -> p (a h f)").bitcast(F32).rearrange("p (h f) -> p h f", h=2)
        w_proj = new_ring[:, 0:2, :].rearrange("p a b -> p (a b)")[:, 0:512]
        proj_bias = new_ring[:, 2:4, :].rearrange("p a b -> p (a b)")[:, 0:512]

        k_centre = k[:, K_CENTRE:K_CENTRE + P]
        k_group = k[:, K_GROUP:K_GROUP + P]
        k_ident = k[:, K_IDENT:K_IDENT + P]
        k_sel = k[:, K_SEL:K_SEL + 2]
        gn_mean, gn_dev, gn_q, gn_ve, gn_a, gn_b, gn_cb = (gn[:, i:i + 1] for i in range(7))

        x_loaded = sems("x_loaded", PIECES)
        in_loaded, gate_stored = sems("in_loaded"), sems("gate_stored")
        t_loaded, res_loaded, gate_loaded, new_stored = (
            sems(name, PAIRS) for name in ("t_loaded", "res_loaded", "gate_loaded", "new_stored"))
        planes_stored = sems("planes_stored", 2)
        consts_loaded, params_loaded = sem("consts_loaded"), sem("params_loaded")
        turned_stored = sems("turned_stored", 2)
        consts_ready, shift_ready, bias_mm, params_chain, params_ready = (
            sem("consts_ready"), sem("shift_ready"), sem("bias_mm"), sem("params_chain"), sem("params_ready"))
        mask_ready = sem("mask_ready")
        stats_done, gn_dve, gn_pe, gn_pool = sem("stats_done"), sem("gn_dve"), sem("gn_pe"), sem("gn_pool")
        a_z, a_cen, a_sq, a_var, a_ve, a_rstd, a_rb, a_bc, a_xn = (
            sem("a_" + s) for s in ("z", "cen", "sq", "var", "ve", "rstd", "rb", "bc", "xn"))
        a_hi, a_lo, a_sq_lo = sem("a_hi"), sem("a_lo"), sem("a_sq_lo")
        a_gate_mm, a_gate, a_proj, a_sig, a_free = (
            sem("a_" + s) for s in ("gate_mm", "gate", "proj", "sig", "free"))
        b1_mm, b1_main, b1_tail = sem("b1_mm"), sem("b1_main"), sem("b1_tail")
        b2_z, b2_cen, b2_sq, b2_var, b2_std, b2_rstd, b2_rb, b2_bc, b2_zn = (
            sem("b2_" + s) for s in ("z", "cen", "sq", "var", "std", "rstd", "rb", "bc", "zn"))
        b2_aff, b2_val, b2_out, b2_gated, b2_new, b2_turned = (
            sem("b2_" + s) for s in ("aff", "val", "out", "gated", "new", "turned"))

        def x_src(l):
            return x_in if l == 0 else scratch

        def x_dst(l):
            return x_out if l == LAYERS - 1 else scratch

        def lr_view(l):
            flat = lr[:, :].bitcast(BF16)[:, 0:COLS * N] if l == 0 else lr[:, :]
            return flat.rearrange("p (c r) -> p c r", r=N)

        turned = lr[:, 0:N * HALF].rearrange("p (j i) -> p j i", i=HALF)

        x_all = lr[:, COLS * N // 2:].rearrange("p (t f) -> p t f", f=TILE)

        def t_dram(l):
            return t_bf16 if l == 0 else t_f32

        def t_tiles(l, n):
            return t_dram(l).rearrange("c (h t f) -> h c t f", h=2, f=TILE)[:, :, bass.ds(n, 2), :]

        def column_parts(l, tile):
            if l != 2:
                return [tile]
            return [tile.rearrange("p (r h i) -> p h r i", h=2, r=ROWS)[:, h, :, :] for h in range(2)]

        def x_parts(l, ring, s):
            if l != 2:
                return [ring[:, s, :]]
            return [ring[:, s, :].rearrange("p (h r i) -> p h r i", h=2, r=ROWS)[:, h, :, :] for h in range(2)]

        def two_tiles(dram, n):
            return dram.rearrange("t p f -> p t f")[:, bass.ds(n, 2), :]

        def t_slots(l, s, count=1):
            if l == 0:
                return in_ring[:, s:s + count, :].bitcast(BF16)[:, :, 0:TILE]
            return in_ring[:, s:s + count, :]

        def plane_out(l, g):
            main = in_ring[:, 2 * g:2 * g + 2, :].rearrange("p a b -> p (a b)")
            tail = cen[:, g, :]
            if l == 0:
                main, tail = main.bitcast(BF16)[:, 0:GROUP * N], tail.bitcast(BF16)[:, 0:2 * N]
            return main.rearrange("p (d q) -> p d q", q=N), tail.rearrange("p (d q) -> p d q", q=N)

        def in_count(l):
            return 16 * TURNS * (l - 1)

        n_params = [4 + HAS_LN[l] + (1 if l < 2 else (2 if HAS_MASK[l] else 0)) for l in range(LAYERS)]

        def params_count(l):
            return 16 * sum(n_params[:l + 1])

        def gated_before(l):
            return sum(TILES for m in range(l) if not GATE_FIRST[m])

        def val_before(l):
            return sum(TILES for m in range(l) if GATE_FIRST[m])

        def parts_before(l):
            return sum(TILES for m in range(l) if IN_PARTS[m])

        def slot_free(eng, semaphore, value):
            if not (isinstance(value, int) and value <= 0):
                eng.wait_ge(semaphore, value)

        def over_tiles(eng, step, reach=RING):
            last = TURNS - reach // RING
            for s in range(RING):
                step(s, 0, s, TILES - 1 - s)
            with eng.Fori(1, last) as i:
                for s in range(RING):
                    step(i * RING + s, i, s, reach)
            for n in range(last * RING, TILES):
                step(n, n // RING, n % RING, TILES - 1 - n)

        block = ctx.enter_context(nc.Block())

        @block.sync
        def _(sp):
            sp.dma_start(k[:, :], consts).then_inc(consts_loaded, 16)

            def load_params(l):
                pr = params[l]
                sp.dma_start(w_proj, pr["w_proj"]).then_inc(params_loaded, 16)
                if HAS_LN[l]:
                    sp.dma_start(proj_bias, pr["proj_bias"]).then_inc(params_loaded, 16)
                for tile, name in ((w_gate, "w_gate"), (w_out, "w_out")):
                    sp.dma_start(tile[:, :], pr[name]).then_inc(params_loaded, 16)
                sp.dma_start(cols[:, l % 2, :], pr["cols"]).then_inc(params_loaded, 16)
                if "mask" in pr:
                    sp.dma_start(mask[:, :, :], pr["mask"]).then_inc(params_loaded, 16)
                elif HAS_MASK[l]:
                    sp.dma_start(mask_k8[:, :], mask3_k).then_inc(params_loaded, 16)
                    sp.dma_start(mask_row8[:, :], mask3_row).then_inc(params_loaded, 16)

            load_params(0)
            for q in range(PIECES):
                tiles = slice(q * TILES // PIECES, (q + 1) * TILES // PIECES)
                sp.dma_start(x_all[:, tiles, :], x_in.rearrange("t p f -> p t f")[:, tiles, :]).then_inc(x_loaded[q], 16)

            def phase_a(l):
                src, used = x_src(l), (a_z if HAS_LN[l] else a_xn)
                lead = RING if HAS_LN[l] else 2

                def load(n, s):
                    sp.dma_start(in_ring[:, s, :], src[n, :, :]).then_inc(in_loaded[s], 16)

                def step(n, i, s, ahead):
                    if l and ahead >= RING + lead:
                        sp.wait_ge(used, l * TILES + n + lead + 1)
                        load(n + lead + RING, (s + lead) % RING)
                    sp.wait_ge(a_gate, l * TILES + n + 1)
                    sp.dma_start(gate_dram[n, :, :], gate_ring[:, s, :]).then_inc(gate_stored[s], 16)

                if l:
                    for n in range(RING):
                        load(n, n)
                    for n in range(lead):
                        sp.wait_ge(used, l * TILES + n + 1)
                        load(RING + n, n)
                over_tiles(sp, step, 2 * RING)

            def phase_b1(l):
                dram = t_dram(l).rearrange("(g d) (i j) -> g i d j", d=GROUP, j=N)
                for g in range(GROUPS):
                    main, tail = plane_out(l, g % 2)
                    sp.wait_ge(b1_main, l * GROUPS + g + 1)
                    sp.dma_start(dram[g, 0:P, :, :], main).then_inc(planes_stored[g % 2], 16)
                    sp.wait_ge(b1_tail, l * GROUPS + g + 1)
                    for e in range(2):
                        sp.dma_start(dram[g, P:N, e::2, :], tail[TAIL * e:TAIL * e + TAIL, :, :])\
                            .then_inc(planes_stored[g % 2], 16)

            def phase_b2(l):
                src, dst = x_src(l), x_dst(l)
                for s in range(2):
                    sp.wait_ge(planes_stored[s], (l + 1) * 48 * (GROUPS // 2))
                for s in range(RING):
                    sp.wait_ge(gate_stored[s], (l + 1) * 16 * TURNS)

                def load_t(n, s):
                    for h in range(2):
                        sp.dma_start(t_slots(l, s, 2)[C * h:C * h + C, :, :], t_tiles(l, n)[h, :, :, :])\
                            .then_inc(t_loaded[s // 2], 16)

                def load_gate(n, s):
                    sp.dma_start(gate_ring[:, s:s + 2, :], two_tiles(gate_dram, n)).then_inc(gate_loaded[s // 2], 16)

                def load_res(n, s):
                    sp.dma_start(res_ring[:, s:s + 2, :], two_tiles(src, n)).then_inc(res_loaded[s // 2], 16)

                def gate_used(n):
                    if GATE_FIRST[l]:
                        sp.wait_ge(b2_val, val_before(l) + n + 1)
                    else:
                        sp.wait_ge(b2_gated, gated_before(l) + n + 1)

                for n in range(0, RING, 2):
                    load_t(n, n)
                    load_gate(n, n)
                    load_res(n, n)
                for n in range(0, RING, 2):
                    sp.wait_ge(b2_z, l * TILES + n + 2)
                    load_t(RING + n, n)

                def step(n, i, s, ahead):
                    if s % 2 == 0:
                        return
                    if ahead >= 2 * RING:
                        sp.wait_ge(b2_z, l * TILES + n + RING + 1)
                        load_t(n - 1 + 2 * RING, s - 1)
                    if ahead >= RING:
                        gate_used(n)
                        load_gate(n - 1 + RING, s - 1)
                    sp.wait_ge(b2_new, l * TILES + n + 1)
                    if l != 1:
                        sp.dma_start(two_tiles(dst, n - 1), new_ring[:, s - 1:s + 1, :])\
                            .then_inc(new_stored[s // 2], 16)
                    if ahead >= RING:
                        load_res(n - 1 + RING, s - 1)

                over_tiles(sp, step, 2 * RING)
                if l == 1:
                    sp.wait_ge(b2_turned, TILES)
                    quarters = scratch.rearrange("t (h2 c) (h f) -> h h2 c t f", h2=2, h=2)
                    for part, tiles in enumerate((slice(0, EARLY), slice(EARLY, TILES))):
                        for h in range(2):
                            for h2 in range(2):
                                rows = turned[C * h:C * h + C, h2 * HALF:(h2 + 1) * HALF, :]
                                sp.dma_start(quarters[h, h2, :, tiles, :],
                                             rows.rearrange("p (t r) i -> p t (r i)", r=ROWS)[:, tiles, :])\
                                    .then_inc(turned_stored[part], 16)
                    sp.wait_ge(turned_stored[0], 16 * 4)
                else:
                    stores = sum(1 for m in range(l + 1) if m != 1)
                    for s in range(PAIRS):
                        sp.wait_ge(new_stored[s], stores * 16 * TURNS)

            for l in range(LAYERS):
                phase_a(l)
                sp.wait_ge(a_free, (l + 1) * SUBS + 2)
                if l + 1 < LAYERS:
                    load_params(l + 1)
                phase_b1(l)
                phase_b2(l)

        @block.tensor
        def _(pe):
            def params_biases(l):
                pe.wait_ge(params_loaded, params_count(l))
                pe.wait_ge(shift_ready, l + 1)
                if HAS_LN[l]:
                    nc.tensor.matmul(ps[:, 7, 0:512], shift_w[:, :], w_proj, start=True, stop=True)
                nc.tensor.matmul(ps[:, 6, 400:401], w_gate[:, :], shift_col[:, :], start=True, stop=True)
                nc.tensor.matmul(ps[:, 6, 402:403], w_out[:, :], cols[:, l % 2, LN2_B:LN2_B + 1],
                                 start=True, stop=True).then_inc(bias_mm, 1)

            def group_norm(l):
                pe.wait_ge(gn_dve, 7 * l + 1)
                nc.tensor.matmul(ps[:, 6, 0:1], k_group, mv[:, 0:1], start=True, stop=True).then_inc(gn_pe, 1)
                pe.wait_ge(gn_dve, 7 * l + 4)
                nc.tensor.matmul(ps[:, 6, 2:3], k_group, gn_q, start=True, stop=True).then_inc(gn_pe, 1)
                pe.wait_ge(gn_dve, 7 * l + 6)
                nc.tensor.matmul(ps[:, 6, 4:5], k_centre, gn_b, start=True, stop=True).then_inc(gn_pe, 1)

            def phase_a(l):
                base = l * TILES
                ln = HAS_LN[l]
                pe.wait_ge(gn_dve, 7 * (l + 1))
                pe.wait_ge(params_ready, l + 1)

                passes = ((0, 0), (1, 0), (0, 1)) if IN_PARTS[l] else ((0, 0),)

                def moving(part, s):
                    return xn_parts[:, s % 2, part, :] if IN_PARTS[l] else val[:, s % 2, :]

                def gate_weights(part):
                    return w_gate_parts[:, part, :] if IN_PARTS[l] else w_gate[:, :]

                def proj_weights(part, h):
                    return w_parts[:, part, h, :] if IN_PARTS[l] else w_whole[:, h, :]

                def centre(n, i, s):
                    if l:
                        pe.wait_ge(in_loaded[s], in_count(l) + 16 * (i + 1))
                    slot_free(pe, a_sq, base + n - 1)
                    for z, x in zip(column_parts(l, ps[:, s % 2, 0:TILE]),
                                    x_parts(l, in_ring, s) if l else [x_all[:, n, :]]):
                        mm = nc.tensor.matmul(z, w_centre[:, :], x, start=True, stop=True)
                    mm.then_inc(a_z, 1)

                def variance(n, s):
                    pe.wait_ge(a_sq_lo, base + n + 1)
                    slot_free(pe, a_xn, base + n - 1)
                    for j in range(CHUNKS):
                        for part in range(2):
                            mm = nc.tensor.matmul(ps[:, 2, TILE + 2 * j:TILE + 2 * j + 2],
                                                  sq_parts[:, s % 2, part, P * j:P * j + P], sel_bf[:, :],
                                                  start=part == 0, stop=part == 1)
                    mm.then_inc(a_var, 1)

                def spread(n, s, newest):
                    pe.wait_ge(a_rb, base + n + 1)
                    pe.wait_ge(a_ve, base + newest + 1)
                    for j in range(CHUNKS):
                        mm = nc.tensor.transpose(ps[:, 2, P * j:P * j + P], rb[:, s % 2, P * j:P * j + P], k_ident)
                    mm.then_inc(a_bc, 1)

                def gate(n, s):
                    if IN_PARTS[l]:
                        pe.wait_ge(a_lo, parts_before(l) + n + 1)
                    else:
                        pe.wait_ge(a_hi, base + n + 1)
                    slot_free(pe, a_gate, base + n)
                    for w, x in passes:
                        mm = nc.tensor.matmul(ps[:, 3, 0:TILE], gate_weights(w), moving(x, s),
                                              start=(w, x) == passes[0], stop=(w, x) == passes[-1])
                    mm.then_inc(a_gate_mm, 1)

                def project(n, s, r):
                    m = ROWS * n + r
                    pe.wait_ge(a_free, l * SUBS + m + 1)
                    banks = [ps[:, 4 + 2 * r + h, 0:2 * COLS].rearrange("p (v c) -> p v c", v=2) for h in range(2)]
                    for w, x in passes:
                        start, stop = (w, x) == passes[0], (w, x) == passes[-1]
                        for h in range(2):
                            nc.tensor.matmul(banks[h][:, :, 0:P], moving(x, s)[:, N * r:N * r + P],
                                             proj_weights(w, h)[:, 0:2 * P], start=start, stop=stop,
                                             skip_group_check=True)
                    for w, x in passes:
                        start, stop = (w, x) == passes[0], (w, x) == passes[-1]
                        for h in range(2):
                            for e in range(2):
                                mm = nc.tensor.matmul(banks[h][TAIL * e:TAIL * e + TAIL, :, P:COLS],
                                                      moving(x, s)[:, N * r + P:N * r + N],
                                                      proj_weights(w, h)[:, 2 * P + P * e:3 * P + P * e],
                                                      start=start, stop=stop, skip_group_check=True)
                    mm.then_inc(a_proj, 1)

                def step(n, i, s, ahead):
                    gate(n, s)
                    project(n, s, 0)
                    if ln and ahead >= 1:
                        spread(n + 1, (s + 1) % RING, n + min(ahead, 2))
                    if ln and ahead >= 4:
                        centre(n + 4, i + 1, s)
                    project(n, s, 1)
                    if ln and ahead >= 3:
                        variance(n + 3, (s + 3) % RING)

                if ln:
                    for n in range(4):
                        centre(n, 0, n)
                    variance(0, 0)
                    pe.wait_ge(a_ve, base + 1)
                    variance(1, 1)
                    spread(0, 0, 1)
                    variance(2, 2)
                over_tiles(pe, step)

            def keep_clock(bank, count):
                for _ in range(count):
                    nc.tensor.matmul(ps[:, bank, 0:TILE], k_centre, k[:, 0:TILE], start=True, stop=True)

            def phase_b1(l):
                v = lr_view(l)
                pe.wait_ge(a_free, (l + 1) * SUBS + 2)

                def main_lr(d):
                    return v[:, d, :], v[:, C + d, :]

                def tail_lr(d):
                    e = d % 2
                    return (v[TAIL * e:TAIL * e + TAIL, 2 * C + d // 2, :],
                            v[TAIL * e:TAIL * e + TAIL, 2 * C + C // 2 + d // 2, :])

                for g in range(GROUPS):
                    if g == GROUPS // 2 and l + 1 < LAYERS:
                        params_biases(l + 1)
                    b = 3 * (g % 2)
                    if g >= 2:
                        pe.wait_ge(b1_main, l * GROUPS + g - 1)
                        pe.wait_ge(b1_tail, l * GROUPS + g - 1)
                    for part, first in ((main_lr, True), (tail_lr, False)):
                        for pair in range(2):
                            q = slice(N * pair, N * pair + N)
                            start, stop = first and pair == 0, not first and pair == 1
                            even, odd = GROUP * g + 2 * pair, GROUP * g + 2 * pair + 1
                            for e, d in enumerate((even, odd)):
                                left, right = part(d)
                                nc.tensor.matmul(ps[:, b + e, q], left[:, 0:P], right, start=start, stop=stop,
                                                 skip_group_check=True)
                            for e, d in enumerate((even, odd)):
                                left, right = part(d)
                                mm = nc.tensor.matmul(ps[TAIL * e:TAIL * e + TAIL, b + 2, q], left[:, P:N], right,
                                                      start=start, stop=stop, skip_group_check=True)
                    mm.then_inc(b1_mm, 1)

            def phase_b2(l):
                base = l * TILES
                w_c = centre_bf[:, :] if l == 0 else k_centre

                def centre(n, i, s):
                    pe.wait_ge(t_loaded[s // 2], 32 * (l * TURNS + i + 1))
                    slot_free(pe, b2_sq, base + n - 1)
                    nc.tensor.matmul(ps[:, s % 2, 0:TILE], w_c, t_slots(l, s)[:, 0, :],
                                     start=True, stop=True).then_inc(b2_z, 1)

                def variance(n, s):
                    pe.wait_ge(b2_sq, base + n + 1)
                    slot_free(pe, b2_std, base + n - 1)
                    for j in range(CHUNKS):
                        mm = nc.tensor.matmul(ps[:, 6 + s % 2, 2 * j:2 * j + 2],
                                              sq[:, s % 2, P * j:P * j + P], k_sel, start=True, stop=True)
                    mm.then_inc(b2_var, 1)

                def spread(n, s):
                    pe.wait_ge(b2_rb, base + n + 1)
                    slot_free(pe, b2_zn, base + n - 1)
                    for j in range(CHUNKS):
                        mm = nc.tensor.transpose(ps[:, 2 + s % 2, P * j:P * j + P], rb[:, s % 2, P * j:P * j + P],
                                                 k_ident)
                    mm.then_inc(b2_bc, 1)

                def out(n, s):
                    if GATE_FIRST[l]:
                        pe.wait_ge(b2_val, val_before(l) + n + 1)
                    else:
                        pe.wait_ge(b2_zn, base + n + 1)
                    if GATE_FIRST[l]:
                        slot_free(pe, b2_new, base + n - 1)
                    else:
                        slot_free(pe, b2_gated, gated_before(l) + n - 1)
                    if l == 0 and isinstance(n, int) and n < RING:
                        keep_clock(4 + s % 2, 2)
                    nc.tensor.matmul(ps[:, 4 + s % 2, 0:TILE], w_out_s[:, l % 2, :],
                                     (val if GATE_FIRST[l] else xn)[:, s % 2, :], start=True, stop=True)\
                        .then_inc(b2_out, 1)

                lead = 0 if GATE_FIRST[l] else 1

                def step(n, i, s, ahead):
                    if ahead >= 3:
                        variance(n + 3, (s + 3) % RING)
                    if ahead >= 5:
                        centre(n + 5, i + (s + 5) // RING, (s + 5) % RING)
                    if ahead >= 2:
                        spread(n + 2, (s + 2) % RING)
                    if ahead >= lead:
                        out(n + lead, (s + lead) % RING)

                if l + 1 < LAYERS:
                    pe.wait_ge(params_ready, l + 2)
                pe.wait_ge(b1_main, (l + 1) * GROUPS)
                keep_clock(4, 10)
                for n in range(4):
                    centre(n, 0, n)
                keep_clock(4, 1)
                variance(0, 0)
                keep_clock(4, 1)
                variance(1, 1)
                spread(0, 0)
                keep_clock(4, 1)
                centre(4, 1, 0)
                spread(1, 1)
                variance(2, 2)
                if lead:
                    out(0, 0)
                over_tiles(pe, step, 2 * RING)

            pe.wait_ge(consts_ready, 1)
            params_biases(0)
            group_norm(0)
            for l in range(LAYERS):
                phase_a(l)
                phase_b1(l)
                phase_b2(l)
                if l + 1 < LAYERS:
                    group_norm(l + 1)

        @block.scalar
        def _(act):
            def phase_a(l):
                base = l * TILES
                ln = HAS_LN[l]
                act.wait_ge(gn_dve, 7 * (l + 1))
                act.wait_ge(params_ready, l + 1)

                def centred(n, s):
                    act.wait_ge(a_z, base + n + 1)
                    slot_free(act, a_xn, base + n - RING + 1)
                    slot_free(act, a_var, base + n - 1)
                    nc.scalar.activation(cen[:, s, :], ps[:, s % 2, 0:TILE], ACT.Identity, bias=gn_cb)\
                        .then_inc(a_cen, 1)
                    nc.scalar.activation(sq[:, s % 2, :], ps[:, s % 2, 0:TILE], ACT.Square, bias=gn_cb)
                    nc.scalar.activation(sq_parts[:, s % 2, 0, :], ps[:, s % 2, 0:TILE], ACT.Square, bias=gn_cb)\
                        .then_inc(a_sq, 1)

                def spread(n, s):
                    act.wait_ge(a_rstd, base + n + 1)
                    slot_free(act, a_bc, base + n - 1)
                    nc.scalar.activation(rb[:, s % 2, :].rearrange("p (a c) -> p a c", c=C),
                                         rstd[:, s % 2, :].rearrange("p (a o) -> p a o", o=1)
                                         .broadcast_to([P, 2 * CHUNKS, C]), ACT.Copy).then_inc(a_rb, 1)

                def plain(n, i, s):
                    act.wait_ge(in_loaded[s], in_count(l) + 16 * (i + 1))
                    slot_free(act, a_lo, parts_before(l) + n - 1)
                    nc.scalar.activation(xn[:, s % 2, :], in_ring[:, s, :], ACT.Identity, bias=gn_b, scale=gn_a)\
                        .then_inc(a_xn, 1)

                def gate(n, i, s):
                    act.wait_ge(a_gate_mm, base + n + 1)
                    slot_free(act, gate_stored[s], 16 * (l * TURNS + i))
                    nc.scalar.activation(gate_ring[:, s, :], ps[:, 3, 0:TILE], ACT.Sigmoid, bias=gate_bias[:, 0:1])\
                        .then_inc(a_gate, 1)

                def sigmoids(n, s, r):
                    m = ROWS * n + r
                    act.wait_ge(a_proj, l * SUBS + m + 1)
                    act.wait_ge(a_free, l * SUBS + m + 1)
                    nc.scalar.activation(act_out[:, r, :].rearrange("p (h c) -> p h c", h=2),
                                         ps[:, 4 + 2 * r:6 + 2 * r, COLS:2 * COLS], ACT.Sigmoid).then_inc(a_sig, 1)

                def high(n, s):
                    act.wait_ge(a_xn, base + n + 1)
                    slot_free(act, a_proj, l * SUBS + ROWS * (n - 1))
                    out = xn_parts[:, s % 2, 0, :] if IN_PARTS[l] else val[:, s % 2, :]
                    nc.scalar.activation(out, xn[:, s % 2, :], ACT.Copy, bias=1.0 if ln else 0.0).then_inc(a_hi, 1)

                def step(n, i, s, ahead):
                    gate(n, i, s)
                    if not ln and ahead >= 1:
                        high(n + 1, (s + 1) % RING)
                    if not ln and ahead >= 2:
                        plain(n + 2, i + (s + 2) // RING, (s + 2) % RING)
                    sigmoids(n, s, 0)
                    if ln and ahead >= 1:
                        high(n + 1, (s + 1) % RING)
                    if ln and ahead >= 4:
                        centred(n + 4, s)
                    sigmoids(n, s, 1)
                    if ln and ahead >= 2:
                        spread(n + 2, (s + 2) % RING)

                if ln:
                    centred(0, 0)
                    centred(1, 1)
                    spread(0, 0)
                    centred(2, 2)
                    spread(1, 1)
                    centred(3, 3)
                    high(0, 0)
                else:
                    plain(0, 0, 0)
                    high(0, 0)
                    plain(1, 0, 1)
                over_tiles(act, step)

            def phase_b1(l):
                for g in range(GROUPS):
                    main, _ = plane_out(l, g % 2)
                    act.wait_ge(b1_mm, l * GROUPS + g + 1)
                    if g >= 2:
                        act.wait_ge(planes_stored[g % 2], 48 * (l * (GROUPS // 2) + g // 2))
                    b = 3 * (g % 2)
                    nc.scalar.activation(main.rearrange("p (a e) q -> p e a q", e=2),
                                         ps[:, b:b + 2, 0:2 * N].rearrange("p e (a q) -> p e a q", q=N),
                                         ACT.Copy).then_inc(b1_main, 1)

            def phase_b2(l):
                base = l * TILES

                def centred(n, s):
                    act.wait_ge(b2_z, base + n + 1)
                    slot_free(act, b2_zn, base + n - RING + 1)
                    slot_free(act, b2_var, base + n - 1)
                    nc.scalar.activation(cen[:, s, :], ps[:, s % 2, 0:TILE], ACT.Copy, scale=T_SCALE[l])\
                        .then_inc(b2_cen, 1)
                    nc.scalar.activation(sq[:, s % 2, :], ps[:, s % 2, 0:TILE], ACT.Square, scale=T_SCALE[l])\
                        .then_inc(b2_sq, 1)

                def deviation(n, s):
                    act.wait_ge(b2_var, base + n + 1)
                    slot_free(act, b2_rstd, base + n - 1)
                    nc.scalar.activation(ve[:, s % 2, :], ps[:, 6 + s % 2, 0:2 * CHUNKS], ACT.Sqrt,
                                         bias=eps_col[:, :]).then_inc(b2_std, 1)

                def spread(n, s):
                    act.wait_ge(b2_rstd, base + n + 1)
                    slot_free(act, b2_bc, base + n - 1)
                    nc.scalar.activation(rb[:, s % 2, :].rearrange("p (a c) -> p a c", c=C),
                                         rstd[:, s % 2, :].rearrange("p (a o) -> p a o", o=1)
                                         .broadcast_to([P, 2 * CHUNKS, C]), ACT.Copy).then_inc(b2_rb, 1)

                def affine(n, s):
                    act.wait_ge(b2_zn, base + n + 1)
                    slot_free(act, b2_val, val_before(l) + n - 1)
                    nc.scalar.activation(act_out[:, s % 2, :], xn[:, s % 2, :], ACT.Identity,
                                         bias=cols[:, l % 2, LN2_B:LN2_B + 1],
                                         scale=cols[:, l % 2, LN2_W:LN2_W + 1]).then_inc(b2_aff, 1)

                def turn(n, s):
                    act.wait_ge(b2_new, base + n + 1)
                    nc.scalar.activation(turned[:, :, bass.ds(ROWS * n, ROWS)].rearrange("p j i -> p i j"),
                                         new_ring[:, s, :].rearrange("p (r j) -> p r j", r=ROWS),
                                         ACT.Copy).then_inc(b2_turned, 1)

                def step(n, i, s, ahead):
                    if ahead >= 2:
                        spread(n + 2, (s + 2) % RING)
                    if GATE_FIRST[l] and ahead >= 1:
                        affine(n + 1, (s + 1) % RING)
                    if ahead >= 3:
                        deviation(n + 3, (s + 3) % RING)
                    if l == 1 and not (isinstance(n, int) and n == 0):
                        turn(n - 1, (s - 1) % RING)
                    if ahead >= 5:
                        centred(n + 5, (s + 5) % RING)

                nc.scalar.activation(root_table[:, :], eps_col[:, :], ACT.Sqrt)
                centred(0, 0)
                centred(1, 1)
                deviation(0, 0)
                centred(2, 2)
                deviation(1, 1)
                spread(0, 0)
                centred(3, 3)
                spread(1, 1)
                deviation(2, 2)
                centred(4, 0)
                if GATE_FIRST[l]:
                    affine(0, 0)
                over_tiles(act, step, 2 * RING)
                if l == 1:
                    turn(TILES - 1, RING - 1)

            for l in range(LAYERS):
                phase_a(l)
                phase_b1(l)
                phase_b2(l)

        @block.vector
        def _(dve):
            dve.sem_inc(a_free, 2)
            dve.wait_ge(consts_loaded, 16)
            nc.vector.memset(w_parts[:, :, :, :], 0.0)
            nc.vector.memset(averager[:, :], 1 / P)
            nc.vector.memset(eps_col[:, :], LN_EPS)
            nc.vector.tensor_copy(sel_bf[:, :], k_sel)
            nc.vector.tensor_copy(centre_bf[:, :], k_centre).then_inc(consts_ready, 1)

            chain = [0]

            def link(ins):
                chain[0] += 1
                ins.then_inc(params_chain, 1)
                dve.wait_ge(params_chain, chain[0])

            def params_shift(l):
                c = cols[:, l % 2, :]
                dve.wait_ge(params_loaded, params_count(l))
                if l == 0:
                    dve.wait_ge(consts_ready, 1)
                if HAS_LN[l]:
                    link(nc.vector.tensor_tensor(shift_col[:, :], c[:, LN_B:LN_B + 1], c[:, LN_W:LN_W + 1], ALU.subtract))
                    nc.vector.tensor_scalar(shift_w[:, :], averager[:, :], shift_col[:, :], None, ALU.mult)\
                        .then_inc(shift_ready, 1)
                else:
                    nc.vector.memset(shift_col[:, :], 0.0).then_inc(shift_ready, 1)

            def params_scaled(l):
                c = cols[:, l % 2, :]
                dve.wait_ge(bias_mm, l + 1)
                nc.vector.tensor_tensor(gate_bias[:, :], ps[:, 6, 400:401], c[:, GATE_B:GATE_B + 1], ALU.add)
                if HAS_LN[l]:
                    link(nc.vector.scalar_tensor_tensor(proj_bias, proj_bias, 1 / C, ps[:, 7, 0:512],
                                                        ALU.mult, ALU.add))
                    nc.vector.scalar_tensor_tensor(w_proj, w_proj, c[:, LN_W:LN_W + 1], proj_bias, ALU.mult, ALU.add)
                    link(nc.vector.tensor_scalar(w_gate[:, :], w_gate[:, :], c[:, LN_W:LN_W + 1], None, ALU.mult))
                for h in range(2):
                    half = slice(C * h, C * h + C)
                    hi = w_parts[half, 0, h, :] if IN_PARTS[l] else w_whole[half, h, :]
                    nc.vector.tensor_copy(hi, w_proj[half, :])
                if IN_PARTS[l]:
                    if not IN_PARTS[l - 1]:
                        for h in range(2):
                            nc.vector.memset(w_parts[C - C * h:2 * C - C * h, :, h, :], 0.0)
                    link(nc.vector.tensor_copy(w_gate_parts[:, 0, :], w_gate[:, :]))
                    for h in range(2):
                        half = slice(C * h, C * h + C)
                        nc.vector.tensor_tensor(w_parts[half, 1, h, :], w_proj[half, :], w_parts[half, 0, h, :],
                                                ALU.subtract)
                    link(nc.vector.tensor_tensor(w_gate_parts[:, 1, :], w_gate[:, :], w_gate_parts[:, 0, :],
                                                 ALU.subtract))
                if HAS_MASK[l] and l >= 2:
                    nc.vector.tensor_copy(mask_k[:, :], mask_k8[:, :]).then_inc(mask_ready, 1)
                    dve.wait_ge(mask_ready, 1)
                    for t in range(2):
                        nc.vector.tensor_scalar(mask[:, t, :], mask_row8[:, :], mask_k[:, t:t + 1], None, ALU.mult)
                if GATE_FIRST[l]:
                    nc.vector.tensor_copy(out_bias[:, l % 2:l % 2 + 1], c[:, OUT_B:OUT_B + 1])
                    nc.vector.tensor_copy(w_out_s[:, l % 2, :], w_out[:, :]).then_inc(params_ready, 1)
                else:
                    nc.vector.tensor_tensor(out_bias[:, l % 2:l % 2 + 1], ps[:, 6, 402:403], c[:, OUT_B:OUT_B + 1], ALU.add)
                    nc.vector.tensor_scalar(w_out_s[:, l % 2, :], w_out[:, :], c[:, LN2_W:LN2_W + 1], None,
                                            ALU.mult).then_inc(params_ready, 1)

            def group_norm(l):
                b = 7 * l
                dve.wait_ge(stats_done, (l + 1) * TILES)
                nc.vector.bn_aggr(mv[:, :], stats[:, :, :].rearrange("p t s -> p (t s)")).then_inc(gn_dve, 1)
                dve.wait_ge(gn_pe, 3 * l + 1)
                nc.vector.tensor_copy(gn_mean, ps[:, 6, 0:1]).then_inc(gn_dve, 1)
                dve.wait_ge(gn_dve, b + 2)
                nc.vector.tensor_tensor(gn_dev, mv[:, 0:1], gn_mean, ALU.subtract).then_inc(gn_dve, 1)
                dve.wait_ge(gn_dve, b + 3)
                nc.vector.scalar_tensor_tensor(gn_q, gn_dev, gn_dev, mv[:, 1:2], ALU.mult, ALU.add).then_inc(gn_dve, 1)
                dve.wait_ge(gn_pe, 3 * l + 2)
                nc.vector.tensor_scalar(gn_ve, ps[:, 6, 2:3], GN_EPS, None, ALU.add).then_inc(gn_dve, 1)
                dve.wait_ge(gn_pool, l + 1)
                nc.vector.tensor_scalar(gn_b, gn_mean, gn_a, -1.0, ALU.mult, ALU.mult).then_inc(gn_dve, 1)
                nc.vector.tensor_scalar(w_centre[:, :], k_centre, gn_a, None, ALU.mult)
                dve.wait_ge(gn_pe, 3 * l + 3)
                nc.vector.tensor_copy(gn_cb, ps[:, 6, 4:5]).then_inc(gn_dve, 1)

            def phase_a(l):
                base = l * TILES
                ln = HAS_LN[l]
                out4 = lr_view(l).rearrange("p c (h r) -> p h c r", h=2)
                mask4 = mask[:, :, :].rearrange("p t (h r) -> p t h r", h=2)
                if l:
                    dve.wait_ge(b1_mm, l * GROUPS)
                if l == 2:
                    for part in range(2):
                        dve.wait_ge(turned_stored[part], 16 * 4)

                def square_low(n, s):
                    dve.wait_ge(a_sq, base + n + 1)
                    nc.vector.tensor_tensor(sq_parts[:, s % 2, 1, :], sq[:, s % 2, :], sq_parts[:, s % 2, 0, :],
                                            ALU.subtract).then_inc(a_sq_lo, 1)

                def var_eps(n, s):
                    dve.wait_ge(a_var, base + n + 1)
                    slot_free(dve, a_rstd, base + n - 1)
                    nc.vector.tensor_scalar(ve[:, s % 2, :], ps[:, 2, TILE:TILE + 2 * CHUNKS], LN_EPS, None,
                                            ALU.add).then_inc(a_ve, 1)

                def normalise(n, s):
                    dve.wait_ge(a_bc, base + n + 1)
                    dve.wait_ge(a_cen, base + n + 1)
                    if IN_PARTS[l]:
                        slot_free(dve, a_lo, parts_before(l) + n - 1)
                    else:
                        slot_free(dve, a_hi, base + n - 1)
                    nc.vector.tensor_tensor(xn[:, s % 2, :], ps[:, 2, 0:TILE], cen[:, s, :], ALU.mult)\
                        .then_inc(a_xn, 1)

                def low(n, s):
                    dve.wait_ge(a_hi, base + n + 1)
                    nc.vector.scalar_tensor_tensor(xn_parts[:, s % 2, 1, :], xn[:, s % 2, :], 1.0 if ln else 0.0,
                                                   xn_parts[:, s % 2, 0, :], ALU.add, ALU.subtract).then_inc(a_lo, 1)

                def glu(n, r):
                    m = ROWS * n + r
                    dve.wait_ge(a_sig, l * SUBS + m + 1)
                    sig = act_out[:, r, :].rearrange("p (h c) -> p h c", h=2)
                    if HAS_MASK[l]:
                        for h in range(2):
                            for t, (lo, hi) in enumerate(((0, P), (P, COLS))):
                                ins = nc.vector.scalar_tensor_tensor(
                                    out4[:, h, lo:hi, m], ps[:, 4 + 2 * r + h, lo:hi], mask4[:, t, h, bass.ds(m, 1)],
                                    sig[:, h, lo:hi], ALU.mult, ALU.mult)
                        ins.then_inc(a_free, 1)
                    else:
                        nc.vector.tensor_tensor(out4[:, :, :, m], ps[:, 4 + 2 * r:6 + 2 * r, 0:COLS], sig,
                                                ALU.mult).then_inc(a_free, 1)

                def step(n, i, s, ahead):
                    if ln and ahead >= 2:
                        var_eps(n + 2, (s + 2) % RING)
                    if not (isinstance(n, int) and n == 0):
                        glu(n - 1, 1)
                    if ln and ahead >= 1:
                        normalise(n + 1, (s + 1) % RING)
                    if ln and ahead >= 3:
                        square_low(n + 3, (s + 3) % RING)
                    if IN_PARTS[l] and ahead >= 1:
                        low(n + 1, (s + 1) % RING)
                    glu(n, 0)

                if ln:
                    square_low(0, 0)
                    square_low(1, 1)
                    var_eps(0, 0)
                    var_eps(1, 1)
                    normalise(0, 0)
                    square_low(2, 2)
                if IN_PARTS[l]:
                    low(0, 0)
                over_tiles(dve, step)
                glu(TILES - 1, 1)

            def phase_b1(l):
                for g in range(GROUPS):
                    if g == GROUPS // 4 and l + 1 < LAYERS:
                        params_shift(l + 1)
                    if g == GROUPS // 2 + 1 and l + 1 < LAYERS:
                        params_scaled(l + 1)
                    _, tail = plane_out(l, g % 2)
                    dve.wait_ge(b1_mm, l * GROUPS + g + 1)
                    if g >= 2:
                        dve.wait_ge(planes_stored[g % 2], 48 * (l * (GROUPS // 2) + g // 2))
                    nc.vector.tensor_copy(tail, ps[:, 3 * (g % 2) + 2, 0:2 * N].rearrange("p (a q) -> p a q", q=N))\
                        .then_inc(b1_tail, 1)

            def phase_b2(l):
                base = l * TILES

                def inverse(n, s):
                    dve.wait_ge(b2_std, base + n + 1)
                    slot_free(dve, b2_rb, base + n - 1)
                    nc.vector.reciprocal(rstd[:, s % 2, :], ve[:, s % 2, :]).then_inc(b2_rstd, 1)

                def normalise(n, s):
                    dve.wait_ge(b2_bc, base + n + 1)
                    dve.wait_ge(b2_cen, base + n + 1)
                    if GATE_FIRST[l]:
                        slot_free(dve, b2_aff, val_before(l) + n - 1)
                    else:
                        slot_free(dve, b2_out, base + n - 1)
                    nc.vector.tensor_tensor(xn[:, s % 2, :], ps[:, 2 + s % 2, 0:TILE], cen[:, s, :], ALU.mult)\
                        .then_inc(b2_zn, 1)

                def finish(n, i, s):
                    bias = out_bias[:, l % 2:l % 2 + 1]
                    dve.wait_ge(b2_out, base + n + 1)
                    if GATE_FIRST[l]:
                        dve.wait_ge(res_loaded[s // 2], 16 * (l * TURNS + i + 1))
                        slot_free(dve, new_stored[s // 2], 16 * (l // 2 * TURNS + i))
                        for new, out, res in zip(column_parts(l, new_ring[:, s, :]),
                                                 column_parts(l, ps[:, 4 + s % 2, 0:TILE]), x_parts(l, res_ring, s)):
                            ins = nc.vector.scalar_tensor_tensor(new, out, bias, res, ALU.add, ALU.add)
                        ins.then_inc(b2_new, 1)
                    else:
                        dve.wait_ge(gate_loaded[s // 2], 16 * (l * TURNS + i + 1))
                        slot_free(dve, b2_new, base + n - 1)
                        nc.vector.scalar_tensor_tensor(val[:, s % 2, :], ps[:, 4 + s % 2, 0:TILE], bias,
                                                       gate_ring[:, s, :], ALU.add, ALU.mult).then_inc(b2_gated, 1)

                def statistics(n, s):
                    dve.wait_ge(b2_new, base + n + 1)
                    nc.vector.bn_stats(stats[:, n, :], new_ring[:, s, :]).then_inc(stats_done, 1)

                lead = 0 if GATE_FIRST[l] else 1

                def step(n, i, s, ahead):
                    if ahead >= 3:
                        inverse(n + 3, (s + 3) % RING)
                    if ahead >= 2:
                        normalise(n + 2, (s + 2) % RING)
                    if not (isinstance(n, int) and n == 0) and l + 1 < LAYERS:
                        statistics(n - 1, (s - 1) % RING)
                    if ahead >= lead:
                        finish(n + lead, i + (s + lead) // RING, (s + lead) % RING)

                inverse(0, 0)
                inverse(1, 1)
                normalise(0, 0)
                normalise(1, 1)
                inverse(2, 2)
                if lead:
                    finish(0, 0, 0)
                over_tiles(dve, step)
                if l + 1 < LAYERS:
                    statistics(TILES - 1, RING - 1)

            params_shift(0)
            params_scaled(0)
            for q in range(PIECES):
                dve.wait_ge(x_loaded[q], 16)
                with dve.Fori(q * TURNS // PIECES, (q + 1) * TURNS // PIECES) as i:
                    for s in range(RING):
                        n = i * RING + s
                        nc.vector.bn_stats(stats[:, n, :], x_all[:, n, :]).then_inc(stats_done, 1)
            group_norm(0)
            for l in range(LAYERS):
                phase_a(l)
                phase_b1(l)
                phase_b2(l)
                if l + 1 < LAYERS:
                    group_norm(l + 1)

        @block.gpsimd
        def _(pool):
            half_set = sem("half_set")
            nc.gpsimd.memset(half_col[:, :], -0.5).then_inc(half_set, 1)
            pool.wait_ge(half_set, 1)

            def group_norm(l):
                pool.wait_ge(gn_dve, 7 * l + 5)
                nc.gpsimd.tensor_tensor(gn_a, gn_ve, half_col[:, 0:1], ALU.pow).then_inc(gn_pool, 1)

            def phase_a(l):
                base = l * TILES
                ln = HAS_LN[l]

                def inverse(n, s):
                    pool.wait_ge(a_ve, base + n + 1)
                    slot_free(pool, a_rb, base + n - 1)
                    nc.gpsimd.tensor_tensor(rstd[:, s % 2, :], ve[:, s % 2, :], half_col[:, :], ALU.pow)\
                        .then_inc(a_rstd, 1)

                def step(n, i, s, ahead):
                    if ahead >= 2:
                        inverse(n + 2, (s + 2) % RING)

                if ln:
                    inverse(0, 0)
                    inverse(1, 1)
                    over_tiles(pool, step)

            def phase_b2(l):
                base = l * TILES

                def gated(n, i, s):
                    pool.wait_ge(b2_aff, val_before(l) + n + 1)
                    pool.wait_ge(gate_loaded[s // 2], 16 * (l * TURNS + i + 1))
                    slot_free(pool, b2_out, base + n - 1)
                    nc.gpsimd.tensor_tensor(val[:, s % 2, :], act_out[:, s % 2, :], gate_ring[:, s, :], ALU.mult)\
                        .then_inc(b2_val, 1)

                def residual(n, i, s):
                    pool.wait_ge(b2_gated, gated_before(l) + n + 1)
                    pool.wait_ge(res_loaded[s // 2], 16 * (l * TURNS + i + 1))
                    if l == 1:
                        slot_free(pool, b2_turned, n - RING + 1)
                        slot_free(pool, stats_done, (l + 1) * TILES + n - RING + 1)
                    else:
                        pool.wait_ge(new_stored[s // 2], 16 * (2 * TURNS + i))
                    nc.gpsimd.tensor_tensor(new_ring[:, s, :], val[:, s % 2, :], res_ring[:, s, :], ALU.add)\
                        .then_inc(b2_new, 1)

                def step(n, i, s, ahead):
                    if not GATE_FIRST[l]:
                        residual(n, i, s)
                    elif ahead >= 1:
                        gated(n + 1, i + (s + 1) // RING, (s + 1) % RING)

                if GATE_FIRST[l]:
                    gated(0, 0, 0)
                over_tiles(pool, step)

            group_norm(0)
            for l in range(LAYERS):
                phase_a(l)
                phase_b2(l)
                if l + 1 < LAYERS:
                    group_norm(l + 1)


def shape_constants():
    import numpy as np
    k = np.zeros((P, NCONST), np.float32)
    part = np.arange(P)
    same_half = part[:, None] // C == part[None, :] // C
    k[:, K_CENTRE:K_CENTRE + P] = np.eye(P) - same_half / C
    k[:, K_GROUP:K_GROUP + P] = (part[:, None] % C // 2 == part[None, :] % C // 2) / 4
    k[:, K_IDENT:K_IDENT + P] = np.eye(P)
    for h in range(2):
        k[C * h:C * h + C, K_SEL + h] = 1 / C
    return k


def kernel(**inputs):
    import numpy as np
    import concourse.bacc as bacc
    from concourse.bass_utils import run_bass_kernel_spmd

    get = {name: np.asarray(a) for name, a in inputs.items()}

    def to_tiles(x):
        return np.ascontiguousarray(x.reshape(2, TILES, ROWS, N, C).transpose(1, 0, 4, 2, 3)).reshape(TILES, P, TILE)

    def blocks(w):
        out = np.zeros((P, P), np.float32)
        out[:C, :C] = w
        out[C:, C:] = w
        return out

    def params(l, left, right, left_g, right_g, gate, out, bias, ln, ln2, gate_b, out_b):
        values, gates = np.concatenate([left, right], 1), np.concatenate([left_g, right_g], 1)
        tails = [[np.concatenate([a[..., e::2], b[..., e::2]], -1) for a, b in ((left, right), (left_g, right_g))]
                 for e in range(2)]
        proj = np.concatenate([values, gates] + tails[0] + tails[1], 1)
        bl, br, blg, brg = bias
        proj_bias = np.concatenate([bl, br, blg, brg] + [b[e::2] for e in range(2) for b in bias])
        ln_w, ln_b = ln
        columns = np.stack([ln_w, ln_b, gate_b, ln2[0], ln2[1], out_b], 1)
        return {"w_proj": np.concatenate([proj, proj], 0), "proj_bias": np.stack([proj_bias] * P),
                "w_gate": blocks(gate), "w_out": blocks(out),
                "cols": np.concatenate([columns, columns], 0)}

    def mask_tiles(m):
        mt = m.reshape(N, N).T
        return np.stack([mt[:P], np.concatenate([mt[P:], mt[P:]], 0)], 1)

    zero, one = np.zeros(C, np.float32), np.ones(C, np.float32)
    a, b, c, d = ({n[8:]: v for n, v in get.items() if n.startswith(f"L{l}_conv_")} for l in range(LAYERS))
    layers = [
        params(0, a["Wl"].T, a["Wr"].T, a["Wlg"].T, a["Wrg"].T, a["Wog"].T, a["Wout"].T, (zero,) * 4,
               (a["ln1_w"], a["ln1_b"]), (a["ln2_w"], a["ln2_b"]), zero, zero),
        params(1, b["w_a_p"], b["w_b_p"], b["w_a_g"], b["w_b_g"], b["w_g"], b["w_o"],
               (b["b_a_p"], b["b_b_p"], b["b_a_g"], b["b_b_g"]),
               (b["ln_in_w"], b["ln_in_b"]), (b["ln_out_w"], b["ln_out_b"]), b["b_g"], b["b_o"]),
        params(2, c["Wl"], c["Wr"], c["Wlg"], c["Wrg"], c["Wog"], c["Wo"],
               (c["bl"], c["br"], c["blg"], c["brg"]),
               (c["norm_a"], c["norm_b"]), (c["on_a"], c["on_b"]), c["bog"], c["bo"]),
        params(3, d["W_lr"][:, 0:C], d["W_lr"][:, C:2 * C], d["W_lr"][:, 2 * C:3 * C], d["W_lr"][:, 3 * C:4 * C],
               d["W_gate"], d["W_out"], (zero,) * 4, (one, zero), (d["ln_w"], d["ln_b"]), zero, zero),
    ]
    layers[0]["mask"] = mask_tiles(a["mask"])
    layers[1]["mask"] = mask_tiles(b["mask"])
    m3 = d["mask"].reshape(N).view(np.uint8)
    mask3_k = np.stack([m3[:P], np.concatenate([m3[P:], m3[P:]])], 1)
    mask3_row = np.stack([m3] * P)

    nc = bacc.Bacc("TRN2", target_bir_lowering=False, num_devices=1)
    arrays = {}

    def dram_in(name, array):
        arrays[name] = np.ascontiguousarray(array)
        return nc.dram_tensor(name, array.shape, mybir.dt.from_np(array.dtype), kind="ExternalInput").ap()

    x_ap = dram_in("x", to_tiles(get["x"][0]))
    del layers[3]["proj_bias"]
    params_ap = [{n: dram_in(f"l{l}_{n}", v) for n, v in layers[l].items()} for l in range(LAYERS)]
    consts_ap = dram_in("consts", shape_constants())
    mask3_k_ap, mask3_row_ap = dram_in("mask3_k", mask3_k), dram_in("mask3_row", mask3_row)
    out_ap = nc.dram_tensor("out", (TILES, P, TILE), F32, kind="ExternalOutput").ap()
    build_triangle_layers(nc, x_ap, params_ap, consts_ap, mask3_k_ap, mask3_row_ap, out_ap)
    r = run_bass_kernel_spmd(nc, [arrays], core_ids=[0])
    out = r.results[0]["out"].reshape(TILES, 2, C, ROWS, N)
    return np.ascontiguousarray(out.transpose(4, 1, 0, 3, 2)).reshape(1, N, N, C)
```
